# Optimizing a Trainium2 kernel written in Bass

```python
import numpy as np
import jax
import jax.numpy as jnp

def _softmax(x, axis=-1):
    return jax.nn.softmax(x, axis=axis)

def _gelu(x):
    return jax.nn.gelu(x, approximate=True)

def _silu(x):
    return jax.nn.silu(x)

def _sigmoid(x):
    return jax.nn.sigmoid(x)

def _layernorm(x, axis=-1, eps=1e-05):
    m = jnp.mean(x, axis=axis, keepdims=True)
    v = jnp.var(x, axis=axis, keepdims=True)
    return (x - m) / jnp.sqrt(v + eps)

def _scatter_add(tgt, idx, src, axis=0):
    return tgt.at[idx].add(src)

def _segment_sum(src, seg, n):
    return jax.ops.segment_sum(src, seg, n)
kernel_name = 'mk_prb_d1_jaxref_r8_850b07'

def setup_inputs(seed: int=0):
    np.random.seed(seed)
    _w = jnp.asarray

    def _L0_attn_setup():
        import jax, jax.numpy as jnp
        import numpy as np
        B, N, DIM, H = (8, 512, 128, 16)
        D = DIM // H
        EPS_NORM = 1e-12
        EPS_PI = 1e-08
        key = jax.random.key(seed)
        k1, k2, k3 = jax.random.split(key, 3)
        x = jax.random.normal(k1, (B, N, DIM), dtype=jnp.float32)
        Wqkv = jax.random.normal(k2, (DIM, DIM), dtype=jnp.float32) * (1.0 / np.sqrt(DIM))
        temp = jnp.ones((H, 1), dtype=jnp.float32)
        Wout = jax.random.normal(k3, (DIM, DIM), dtype=jnp.float32) * (1.0 / np.sqrt(DIM))
        bout = jnp.zeros((DIM,), dtype=jnp.float32)
        return {'x': x, 'Wqkv': Wqkv, 'temp': temp, 'Wout': Wout, 'bout': bout}
    _L0_attn_in = _L0_attn_setup()

    def _L0_ffn_setup():
        import jax, jax.numpy as jnp
        import numpy as np
        B, S, D = (1, 256, 128)
        E, K, F = (8, 2, 176)
        NS = 2
        SCALE = 2.5

        def _swiglu_mlp(x, wg, wu, wd):
            return jax.nn.silu(x @ wg) * (x @ wu) @ wd
        key = jax.random.key(seed)
        ks = jax.random.split(key, 8)
        s = 0.02
        return {'hidden_states': jax.random.normal(ks[0], (B, S, D), jnp.float32), 'gate_w': jax.random.normal(ks[1], (E, D), jnp.float32) * s, 'w_gate': jax.random.normal(ks[2], (E, D, F), jnp.float32) * s, 'w_up': jax.random.normal(ks[3], (E, D, F), jnp.float32) * s, 'w_down': jax.random.normal(ks[4], (E, F, D), jnp.float32) * s, 'sw_gate': jax.random.normal(ks[5], (D, F * NS), jnp.float32) * s, 'sw_up': jax.random.normal(ks[6], (D, F * NS), jnp.float32) * s, 'sw_down': jax.random.normal(ks[7], (F * NS, D), jnp.float32) * s}
    _L0_ffn_in = _L0_ffn_setup()
    _d = {'L0_attn_x': _L0_attn_in['x'], 'L0_attn_Wqkv': _L0_attn_in['Wqkv'], 'L0_attn_temp': _L0_attn_in['temp'], 'L0_attn_Wout': _L0_attn_in['Wout'], 'L0_attn_bout': _L0_attn_in['bout'], 'L0_ffn_gate_w': _L0_ffn_in['gate_w'], 'L0_ffn_w_gate': _L0_ffn_in['w_gate'], 'L0_ffn_w_up': _L0_ffn_in['w_up'], 'L0_ffn_w_down': _L0_ffn_in['w_down'], 'L0_ffn_sw_gate': _L0_ffn_in['sw_gate'], 'L0_ffn_sw_up': _L0_ffn_in['sw_up'], 'L0_ffn_sw_down': _L0_ffn_in['sw_down']}
    _x0 = _d['L0_attn_x']
    _d['L0_attn_x'] = jax.random.normal(jax.random.fold_in(jax.random.key(seed), 1), (32, 256, 128), dtype=_x0.dtype)
    del _x0
    return _d

def reference(L0_attn_x, L0_attn_Wqkv, L0_attn_temp, L0_attn_Wout, L0_attn_bout, L0_ffn_gate_w, L0_ffn_w_gate, L0_ffn_w_up, L0_ffn_w_down, L0_ffn_sw_gate, L0_ffn_sw_up, L0_ffn_sw_down):

    def _L0_attn_ref(x, Wqkv, temp, Wout, bout):
        import jax, jax.numpy as jnp
        import numpy as np
        B, N, DIM, H = (8, 512, 128, 16)
        D = DIM // H
        EPS_NORM = 1e-12
        EPS_PI = 1e-08
        b, n, dim = x.shape
        h, d = (H, dim // H)
        w = (x @ Wqkv.T).reshape(b, n, h, d).transpose(0, 2, 1, 3)
        norm = jnp.sqrt(jnp.sum(w * w, axis=-2, keepdims=True))
        w_normed = w / jnp.maximum(norm, EPS_NORM)
        logits = jnp.sum(w_normed * w_normed, axis=-1) * temp[None, :, :]
        Pi = jax.nn.softmax(logits, axis=1)
        Pi_norm = Pi / (jnp.sum(Pi, axis=-1, keepdims=True) + EPS_PI)
        dots = jnp.einsum('bhn,bhnd->bhd', Pi_norm, w * w)
        attn = 1.0 / (1.0 + dots)
        out = -(w * Pi[..., None]) * attn[:, :, None, :]
        out = out.transpose(0, 2, 1, 3).reshape(b, n, dim)
        return out @ Wout.T + bout

    def _L0_ffn_ref(hidden_states, gate_w, w_gate, w_up, w_down, sw_gate, sw_up, sw_down):
        import jax, jax.numpy as jnp
        import numpy as np
        B, S, D = (1, 256, 128)
        E, K, F = (8, 2, 176)
        NS = 2
        SCALE = 2.5

        def _swiglu_mlp(x, wg, wu, wd):
            return jax.nn.silu(x @ wg) * (x @ wu) @ wd
        identity = hidden_states
        x = hidden_states.reshape(-1, hidden_states.shape[-1])
        T = x.shape[0]
        logits = x.astype(jnp.float32) @ gate_w.astype(jnp.float32).T
        scores = jax.nn.softmax(logits, axis=-1)
        topk_w, topk_i = jax.lax.top_k(scores, K)
        topk_w = topk_w / (topk_w.sum(-1, keepdims=True) + 1e-20) * SCALE
        combine = jnp.zeros((T, E), jnp.float32).at[jnp.arange(T)[:, None], topk_i].set(topk_w)
        g = jax.nn.silu(jnp.einsum('td,edf->etf', x, w_gate)) * jnp.einsum('td,edf->etf', x, w_up)
        expert_out = jnp.einsum('etf,efd->etd', g, w_down)
        y = jnp.einsum('te,etd->td', combine, expert_out).astype(x.dtype)
        y = y.reshape(identity.shape)
        return y + _swiglu_mlp(identity, sw_gate, sw_up, sw_down)
    x = L0_attn_x
    xn = _layernorm(x, axis=-1)
    x = x + _L0_attn_ref(xn, L0_attn_Wqkv, L0_attn_temp, L0_attn_Wout, L0_attn_bout) + _L0_ffn_ref(xn, L0_ffn_gate_w, L0_ffn_w_gate, L0_ffn_w_up, L0_ffn_w_down, L0_ffn_sw_gate, L0_ffn_sw_up, L0_ffn_sw_down)
    return x

_drawn_inputs = setup_inputs


def setup_inputs(seed=0):
    import zlib

    import numpy as np

    out = dict(_drawn_inputs(seed))
    spreads = {'L0_attn_temp': (1.0, 0.6), 'L0_attn_bout': (0.0, 0.1)}
    factors = {'L0_ffn_gate_w': 5.32,
     'L0_ffn_w_gate': 4.68,
     'L0_ffn_w_up': 4.642,
     'L0_ffn_w_down': 4.641,
     'L0_ffn_sw_gate': 5.882,
     'L0_ffn_sw_up': 5.861,
     'L0_ffn_sw_down': 5.871}
    for name, (base, spread) in spreads.items():
        noise = np.random.default_rng([zlib.crc32(name.encode()), seed]).standard_normal(out[name].shape)
        drawn = base * np.exp(spread * noise) if base else spread * noise
        out[name] = jnp.asarray(drawn.astype(out[name].dtype))
    for name, factor in factors.items():
        out[name] = (out[name] * factor).astype(out[name].dtype)
    return out
```

```python
from contextlib import ExitStack

import concourse.bass as bass
from concourse import mybir

ALU = mybir.AluOpType
ACT = mybir.ActivationFunctionType
AX = mybir.AxisListType
F32 = mybir.dt.float32
F16 = mybir.dt.float16
U32 = mybir.dt.uint32

P = 128
BLK = 512
TJ = BLK // P
LN_EPS = 1e-5
NORM_EPS_SQ = 1e-12 ** 2
PI_EPS = 1e-8
TOPK_EPS = 1e-20
ROUTED_SCALE = 2.5
LAG = 3
RING = 4

EXP_MASK = 0x7F800000


def over(k):
    return float((254 + k) << 23)


def attn_moe_kernel(nc, x, Wqkv, temp, Wout, bout, gate_w, w_gate, w_up, w_down, sw_gate, sw_up, sw_down, out):
    NB, N, D = x.shape
    E, _, F = w_gate.shape
    FS = sw_gate.shape[1]
    H = temp.shape[0]
    HD = D // H
    G = NB * N // BLK
    BPG = BLK // N
    ROWS = N // TJ
    KE = F * E // P
    ER = P // E
    NT = KE + -(-FS // P)
    MLAST = FS - (NT - 1 - KE) * P
    assert D == P and F == ER * KE and BPG * ROWS == P and G % 2 == 0 and NT % 2 == 0 and BPG == 2
    WID = NT * P

    x_view = x.rearrange("b n d -> (b n) d").rearrange("(g p j) d -> g p (j d)", p=P, j=TJ)
    out_view = out.rearrange("b n d -> (b n) d").rearrange("(g p j) d -> g p (j d)", p=P, j=TJ)

    with ExitStack() as ctx:
        def sb(name, shape, dt=F32):
            return ctx.enter_context(nc.sbuf_tensor(name, shape, dt))

        def ps(name, shape, dt=F32):
            return ctx.enter_context(nc.psum_tensor(name, shape, dt))

        def sem(name):
            return ctx.enter_context(nc.semaphore(name))

        gate_raw = sb("gate_raw", [P, E * F + FS])
        up_raw = sb("up_raw", [P, E * F + FS])
        down_raw = sb("down_raw", [P, WID])
        qkv_raw = sb("qkv_raw", [P, P])
        out_raw = sb("out_raw", [P, P])
        router_raw = sb("router_raw", [E, P])
        gate_hi = sb("gate_hi", [P, WID], F16)
        gate_lo = sb("gate_lo", [P, WID], F16)
        up_hi = sb("up_hi", [P, WID], F16)
        up_lo = sb("up_lo", [P, WID], F16)
        down_hi = sb("down_hi", [P, WID], F16)
        down_lo = sb("down_lo", [P, WID], F16)
        qkv_hi = sb("qkv_hi", [P, P], F16)
        qkv_lo = sb("qkv_lo", [P, P], F16)
        router_hi = sb("router_hi", [P, E], F16)
        router_lo = sb("router_lo", [P, E], F16)
        qkvT = sb("qkvT", [P, P])
        routerT = sb("routerT", [P, E])
        woutT = sb("woutT", [P, P])
        temp_bc = sb("temp_bc", [P, H])
        bias_col = sb("bias_col", [P, 1])

        ident = sb("ident", [P, P])
        head_sel = sb("head_sel", [P, H])
        before = sb("before", [P, E, E])
        neg_half = sb("neg_half", [P, TJ])
        ln_eps = sb("ln_eps", [P, TJ])
        maxima = sb("maxima", [P, 5])
        max_all = sb("max_all", [P, 5])
        clamped = sb("clamped", [P, 5])
        power = sb("power", [P, 5])
        alpha = sb("alpha", [P, 5])
        inv_alpha = sb("inv_alpha", [P, 5])
        gate_pow = sb("gate_pow", [P, 1])
        beta = sb("beta", [P, 1])
        gamma = sb("gamma", [P, 1])
        inv_gamma = sb("inv_gamma", [P, 1])
        neg_gamma_q = sb("neg_gamma_q", [P, 1])

        x_in = sb("x_in", [P, 2, TJ, P])
        x_res = sb("x_res", [P, 2, BLK])
        stats = sb("stats", [P, TJ, 6])
        mean_var = sb("mean_var", [P, TJ, 2])
        var_eps = sb("var_eps", [P, TJ])
        rstd = sb("rstd", [P, TJ])
        xn = sb("xn", [P, TJ, P])
        xT_hi = sb("xT_hi", [P, 2, BLK], F16)
        xT_lo = sb("xT_lo", [P, 2, BLK], F16)
        w_sq = sb("w_sq", [P, BLK])
        norm_sq = sb("norm_sq", [P, BPG])
        norm_max = sb("norm_max", [P, BPG])
        norm_inv = sb("norm_inv", [P, BPG])
        head_scaled = sb("head_scaled", [P, BPG, H])
        logits = sb("logits", [P, TJ, H + E])
        top = sb("top", [P, TJ, 2])
        shifted = sb("shifted", [P, TJ, H + E])
        expd = sb("expd", [P, TJ, H + E])
        sums = sb("sums", [P, TJ, 2])
        sums_inv = sb("sums_inv", [P, TJ, 2])
        score = sb("score", [P, TJ, E])
        diff = sb("diff", [P, TJ, E, E])
        tied = sb("tied", [P, TJ, E, E])
        ahead = sb("ahead", [P, TJ, E, E])
        rank = sb("rank", [P, TJ, E])
        picked = sb("picked", [P, TJ, E])
        picked_sum = sb("picked_sum", [P, TJ])
        picked_eps = sb("picked_eps", [P, TJ])
        picked_inv = sb("picked_inv", [P, TJ])
        combine = sb("combine", [P, TJ, E])
        pi_wide = sb("pi_wide", [P, TJ, H, HD])
        combine_wide = sb("combine_wide", [P, TJ, E, ER])
        pi_bc = sb("pi_bc", [P, BLK])
        pi_sum = sb("pi_sum", [P, BPG])
        weighted = sb("weighted", [P, BLK])
        dots = sb("dots", [P, BPG])
        attn_den = sb("attn_den", [P, BPG])
        attn_inv = sb("attn_inv", [P, BPG])
        attn = sb("attn", [P, BPG])
        attn_out = sb("attn_out", [P, 2, BLK])
        combine_bc = sb("combine_bc", [P, 2, BLK])

        act_gate = sb("act_gate", [P, RING, BLK])
        hidden = sb("hidden", [P, RING, BLK])
        hid_hi = sb("hid_hi", [P, RING, BLK], F16)
        hid_lo = sb("hid_lo", [P, RING, BLK], F16)
        yT = sb("yT", [P, BLK])
        result = sb("result", [P, 2, BLK])

        ps_gate = ps("ps_gate", [P, 2, BLK])
        ps_up = ps("ps_up", [P, 2, BLK])
        ps_y = ps("ps_y", [P, BLK])
        ps_x = ps("ps_x", [P, BLK])
        ps_w = ps("ps_w", [P, BLK])
        ps_s = ps("ps_s", [P, BLK])

        x_in_loaded = [sem("x_in_loaded0"), sem("x_in_loaded1")]
        x_res_loaded = [sem("x_res_loaded0"), sem("x_res_loaded1")]
        stored = [sem("stored0"), sem("stored1")]
        small_loaded = sem("small_loaded")
        gate_loaded, up_loaded, down_loaded = sem("gate_loaded"), sem("up_loaded"), sem("down_loaded")
        consts_step, consts_done = sem("consts_step"), sem("consts_done")
        setup_transposed = sem("setup_transposed")
        setup_step = sem("setup_step")
        maxima_ready, maxima_spread = sem("maxima_ready"), sem("maxima_spread")
        scales_ready, weights_hi, weights_ready = sem("scales_ready"), sem("weights_hi"), sem("weights_ready")
        dve_step = sem("dve_step")
        pool_step = sem("pool_step")
        stats_ready, rstd_ready, xn_ready = sem("stats_ready"), sem("rstd_ready"), sem("xn_ready")
        xT_ready, hi_x_ready, lo_x_ready = sem("xT_ready"), sem("hi_x_ready"), sem("lo_x_ready")
        w_ready, wsq_ready, head_scaled_ready = sem("w_ready"), sem("wsq_ready"), sem("head_scaled_ready")
        logits_ready, shifted_ready, exp_ready = sem("logits_ready"), sem("shifted_ready"), sem("exp_ready")
        routed, wide_ready, spread_ready = sem("routed"), sem("wide_ready"), sem("spread_ready")
        pi_ready, combine_ready, attn_ready = sem("pi_ready"), sem("combine_ready"), sem("attn_ready")
        gate_ready, up_ready, silu_ready = sem("gate_ready"), sem("up_ready"), sem("silu_ready")
        combined, hid_ready = sem("combined"), sem("hid_ready")
        hid_hi_ready, hid_lo_ready, down_done = sem("hid_hi_ready"), sem("hid_lo_ready"), sem("down_done")
        y_taken, yT_ready, result_ready = sem("y_taken"), sem("yT_ready"), sem("result_ready")

        def count(g, per, k):
            m, c = g
            return m * (2 * per) + (c * per + k)

        def after(g, k=1):
            return count(g, 1, k)

        def loads(g):
            m, c = g
            return m * 16 + 16 * (c // 2 + 1)

        def shift(g, by):
            return (g[0], g[1] + by)

        def fixed(g):
            return isinstance(g[0], int)

        def early(g, n):
            return fixed(g) and 2 * g[0] + g[1] < n

        def batch(ap, b):
            return ap.rearrange("p (j b q) -> p b j q", j=TJ, b=BPG)[:, b]

        def rows(t):
            return MLAST if t == NT - 1 else P

        def rows_of(g):
            return x_view[g[0] * 2 + g[1]], out_view[g[0] * 2 + g[1]]

        def run(eng, first, body):
            body((0, 0), True)
            with eng.Fori(0, (G - 2) // 2) as m:
                body((m, 1), True)
                body((m, 2), True)
            body((0, G - 1), False)

        block = ctx.enter_context(nc.Block())

        @block.sync
        def _(sp):
            def load_x_in(g):
                if not early(g, 2):
                    sp.wait_ge(xn_ready, after(shift(g, -2)))
                sp.dma_start(x_in[:, g[1] % 2].rearrange("p j d -> p (j d)"), rows_of(g)[0]).then_inc(x_in_loaded[g[1] % 2], 16)

            def load_x_res(g):
                if not early(g, 2):
                    sp.wait_ge(result_ready, after(shift(g, -2)))
                sp.dma_start(x_res[:, g[1] % 2], rows_of(g)[0]).then_inc(x_res_loaded[g[1] % 2], 16)

            def store(g):
                sp.wait_ge(result_ready, after(g))
                sp.dma_start(rows_of(g)[1], result[:, g[1] % 2]).then_inc(stored[g[1] % 2], 16)

            load_x_in((0, 0))
            sp.dma_start(gate_raw[:, 0:E * F].rearrange("d (e f) -> d e f", e=E),
                         w_gate.rearrange("e d f -> d e f")).then_inc(gate_loaded, 16)
            sp.dma_start(gate_raw[:, E * F:], sw_gate).then_inc(gate_loaded, 16)
            sp.dma_start(down_raw[:, 0:KE * P], w_down.rearrange("e f d -> (e f) d").rearrange("(p k) d -> p (k d)", k=KE)).then_inc(down_loaded, 16)
            full = FS - MLAST
            sp.dma_start(down_raw[:, KE * P:WID - P].rearrange("p (k d) -> p k d", d=P),
                         sw_down[0:full, :].rearrange("(k p) d -> p k d", p=P)).then_inc(down_loaded, 16)
            sp.dma_start(down_raw[0:MLAST, WID - P:], sw_down[full:, :]).then_inc(down_loaded, 16)
            load_x_in((0, 1))
            load_x_res((0, 0))

            def body(g, more):
                if more and not (fixed(g) and g[1] == G - 1):
                    load_x_in(shift(g, 2)) if not (fixed(g) and g[1] + 2 >= G) else None
                    load_x_res(shift(g, 1))
                if not early(g, 1):
                    store(shift(g, -1))

            body((0, 0), True)
            with sp.Fori(0, (G - 4) // 2) as m:
                body((m, 1), True)
                body((m, 2), True)
            for c in range(G - 3, G):
                body((0, c), True)
            store((0, G - 1))
            for half in stored:
                sp.wait_ge(half, 16 * (G // 2))

        @block.gpsimd
        def _(pool):
            nc.gpsimd.memset(ident[:], 0.0).then_inc(consts_step, 1)
            nc.gpsimd.memset(head_sel[:], 1.0).then_inc(consts_step, 1)
            nc.gpsimd.memset(before[:], 1.0).then_inc(consts_step, 1)
            nc.gpsimd.memset(neg_half[:], -0.5).then_inc(consts_step, 1)
            nc.gpsimd.memset(ln_eps[:], LN_EPS).then_inc(consts_step, 1)
            pool.wait_ge(consts_step, 3)
            nc.gpsimd.affine_select(out=ident[:], in_=ident[:], compare_op=ALU.not_equal, fill=1.0, base=0,
                                    pattern=[[-1, P]], channel_multiplier=1).then_inc(consts_step, 1)
            nc.gpsimd.affine_select(out=before[:], in_=before[:], compare_op=ALU.is_gt, fill=0.0, base=0,
                                    pattern=[[1, E], [-1, E]], channel_multiplier=0).then_inc(consts_step, 1)
            nc.gpsimd.affine_select(out=head_sel[:], in_=head_sel[:], compare_op=ALU.is_ge, fill=0.0, base=0,
                                    pattern=[[-HD, H]], channel_multiplier=1).then_inc(consts_step, 1)
            pool.wait_ge(consts_step, 8)
            nc.gpsimd.affine_select(out=head_sel[:], in_=head_sel[:], compare_op=ALU.is_gt, fill=0.0, base=HD,
                                    pattern=[[HD, H]], channel_multiplier=-1).then_inc(consts_done, 1)

            def layer_norm(g):
                pool.wait_ge(stats_ready, after(g))
                nc.gpsimd.tensor_tensor(var_eps[:], mean_var[:, :, 1], ln_eps[:], ALU.add).then_inc(pool_step, 1)
                pool.wait_ge(pool_step, after(g))
                nc.gpsimd.tensor_tensor(rstd[:], var_eps[:], neg_half[:], ALU.pow).then_inc(rstd_ready, 1)

            def widen(g):
                pool.wait_ge(routed, after(g))
                nc.gpsimd.tensor_tensor(pi_wide[:], expd[:, :, 0:H].unsqueeze(3).broadcast_to([P, TJ, H, HD]),
                                        sums_inv[:, :, 0:1].unsqueeze(3).broadcast_to([P, TJ, H, HD]), ALU.mult)
                nc.gpsimd.tensor_copy(combine_wide[:], combine[:].unsqueeze(3).broadcast_to([P, TJ, E, ER])).then_inc(wide_ready, 1)

            layer_norm((0, 0))
            pool.wait_ge(maxima_ready, 1)
            nc.gpsimd.partition_all_reduce(max_all[:], maxima[:], P, bass.bass_isa.ReduceOp.max).then_inc(maxima_spread, 1)
            widen((0, 0))

            def body(g, more):
                for t in range(KE):
                    pool.wait_ge(silu_ready, count(g, NT, t + 1))
                    if t == 0:
                        pool.wait_ge(combine_ready, after(g))
                    s = act_gate[:, (g[1] * NT + t) % RING]
                    nc.gpsimd.tensor_tensor(s, s, combine_bc[:, g[1] % 2], ALU.mult).then_inc(combined, 1)
                    if t == 1 and more:
                        layer_norm(shift(g, 1))
                    if t == KE - 1 and more:
                        widen(shift(g, 1))

            run(pool, (0, 0), body)

        @block.scalar
        def _(act):
            act.dma_start(qkv_raw[:], Wqkv).then_inc(small_loaded, 16)
            act.dma_start(out_raw[:], Wout).then_inc(small_loaded, 16)
            act.dma_start(router_raw[:], gate_w).then_inc(small_loaded, 16)
            act.dma_start(temp_bc[:], temp.rearrange("h o -> o h").broadcast_to([P, H])).then_inc(small_loaded, 16)
            act.dma_start(bias_col[:], bout.rearrange("(d o) -> d o", o=1)).then_inc(small_loaded, 16)
            act.dma_start(up_raw[:, 0:E * F].rearrange("d (e f) -> d e f", e=E),
                          w_up.rearrange("e d f -> d e f")).then_inc(up_loaded, 16)
            act.dma_start(up_raw[:, E * F:], sw_up).then_inc(up_loaded, 16)

            def split_x(g):
                act.wait_ge(xT_ready, after(g))
                nc.scalar.activation(xT_hi[:, g[1] % 2], ps_x[:], ACT.Copy).then_inc(hi_x_ready, 1)

            def square_w(g):
                act.wait_ge(w_ready, after(g))
                for b in range(BPG):
                    ins = nc.scalar.activation(batch(w_sq[:], b), batch(ps_w[:], b), ACT.Square,
                                               scale=inv_alpha[:, 3:4], accum_out=norm_sq[:, b:b + 1])
                ins.then_inc(wsq_ready, 1)

            def exponentials(g):
                act.wait_ge(shifted_ready, after(g))
                nc.scalar.activation(expd[:], shifted[:], ACT.Exp).then_inc(exp_ready, 1)

            def take_spread(g):
                act.wait_ge(spread_ready, after(g))
                for b in range(BPG):
                    ins = nc.scalar.activation(batch(pi_bc[:], b), batch(ps_x[:], b), ACT.Copy,
                                               accum_out=pi_sum[:, b:b + 1])
                ins.then_inc(pi_ready, 1)
                nc.scalar.activation(combine_bc[:, g[1] % 2], ps_s[:], ACT.Copy).then_inc(combine_ready, 1)

            def take_y(g):
                act.wait_ge(down_done, count(g, NT, NT))
                if not early(g, 1):
                    act.wait_ge(yT_ready, after(g, 0))
                nc.scalar.activation(yT[:], ps_y[:], ACT.Identity, bias=bias_col[:, 0:1],
                                     scale=inv_gamma[:, 0:1]).then_inc(y_taken, 1)

            def split_hidden(g, t):
                m = rows(t)
                act.wait_ge(hid_ready, count(g, NT, t + 1))
                if not (early(g, 1) and t < RING):
                    act.wait_ge(down_done, count(g, NT, t + 1 - RING))
                r = (g[1] * NT + t) % RING
                nc.scalar.activation(hid_hi[0:m, r], hidden[0:m, r], ACT.Copy).then_inc(hid_hi_ready, 1)

            split_x((0, 0))
            act.wait_ge(scales_ready, 1)
            cols = E * F
            act.wait_ge(gate_loaded, 32)
            nc.scalar.activation(gate_hi[:, 0:cols].rearrange("d (k p) -> d k p", k=KE),
                                 gate_raw[:, 0:cols].rearrange("d (p k) -> d k p", k=KE), ACT.Copy, scale=alpha[:, 0:1])
            nc.scalar.activation(gate_hi[:, cols:cols + FS], gate_raw[:, cols:], ACT.Copy, scale=alpha[:, 0:1]).then_inc(weights_hi, 1)
            act.wait_ge(up_loaded, 32)
            nc.scalar.activation(up_hi[:, 0:cols].rearrange("d (k p) -> d k p", k=KE),
                                 up_raw[:, 0:cols].rearrange("d (p k) -> d k p", k=KE), ACT.Copy, scale=alpha[:, 1:2])
            nc.scalar.activation(up_hi[:, cols:cols + FS], up_raw[:, cols:], ACT.Copy, scale=alpha[:, 1:2]).then_inc(weights_hi, 1)
            act.wait_ge(down_loaded, 48)
            nc.scalar.activation(down_hi[:], down_raw[:], ACT.Copy, scale=alpha[:, 2:3]).then_inc(weights_hi, 1)
            square_w((0, 0))
            exponentials((0, 0))
            take_spread((0, 0))

            def body(g, more):
                for t in range(NT):
                    if t == LAG and not early(g, 1):
                        take_y(shift(g, -1))
                    act.wait_ge(gate_ready, count(g, NT, t + 1))
                    if not (early(g, 1) and t < RING):
                        act.wait_ge(hid_ready, count(g, NT, t + 1 - RING))
                    n = g[1] * NT + t
                    m = rows(t)
                    nc.scalar.activation(act_gate[0:m, n % RING], ps_gate[0:m, n % 2], ACT.Silu,
                                         scale=inv_alpha[0:m, 0:1]).then_inc(silu_ready, 1)
                    if t >= 1:
                        split_hidden(g, t - 1)
                    elif not early(g, 1):
                        split_hidden(shift(g, -1), NT - 1)
                    if more:
                        if t == 4:
                            split_x(shift(g, 1))
                        if t == 6:
                            square_w(shift(g, 1))
                        if t == 9:
                            exponentials(shift(g, 1))
                        if t == 12:
                            take_spread(shift(g, 1))

            run(act, (0, 0), body)
            split_hidden((0, G - 1), NT - 1)
            take_y((0, G - 1))

        @block.vector
        def _(dve):
            dve_per_group = 20
            step = [0]

            def link(ins, g):
                step[0] += 1
                ins.then_inc(dve_step, 1)
                dve.wait_ge(dve_step, count(g, dve_per_group, step[0]))

            def bare(ins):
                step[0] += 1
                ins.then_inc(dve_step, 1)

            set_up = [0]

            def setup_link(ins):
                set_up[0] += 1
                ins.then_inc(setup_step, 1)
                dve.wait_ge(setup_step, set_up[0])

            def statistics(g):
                step[0] = 0
                dve.wait_ge(x_in_loaded[g[1] % 2], loads(g))
                for j in range(TJ):
                    ins = nc.vector.bn_stats(stats[:, j], x_in[:, g[1] % 2, j])
                bare(ins)

            def statistics_written(g):
                dve.wait_ge(dve_step, count(g, dve_per_group, 1))

            def mean_variance():
                for j in range(TJ):
                    ins = nc.vector.bn_aggr(mean_var[:, j], stats[:, j])
                ins.then_inc(stats_ready, 1)

            def normalise(g):
                dve.wait_ge(rstd_ready, after(g))
                for j in range(TJ):
                    ins = nc.vector.tensor_scalar(xn[:, j], x_in[:, g[1] % 2, j], mean_var[:, j, 0:1], rstd[:, j:j + 1],
                                                  ALU.subtract, ALU.mult)
                ins.then_inc(xn_ready, 1)

            def rest_x(g):
                dve.wait_ge(hi_x_ready, after(g))
                nc.vector.tensor_tensor(xT_lo[:, g[1] % 2], ps_x[:], xT_hi[:, g[1] % 2], ALU.subtract).then_inc(lo_x_ready, 1)

            def head_scales(g):
                dve.wait_ge(wsq_ready, after(g))
                link(nc.vector.tensor_scalar(norm_max[:], norm_sq[:], NORM_EPS_SQ, None, ALU.max), g)
                link(nc.vector.reciprocal(norm_inv[:], norm_max[:]), g)
                for b in range(BPG):
                    ins = nc.vector.tensor_scalar(head_scaled[:, b], head_sel[:], norm_inv[:, b:b + 1], None, ALU.mult)
                ins.then_inc(head_scaled_ready, 1)

            def shift_logits(g):
                dve.wait_ge(logits_ready, after(g))
                raw = ps_s[:, 0:TJ * BPG * H].rearrange("p (j b h) -> p j b h", j=TJ, b=BPG)
                for b in range(BPG):
                    r = slice(b * ROWS, (b + 1) * ROWS)
                    nc.vector.tensor_copy(logits[r, :, 0:H], raw[r, :, b])
                ins = nc.vector.tensor_scalar(logits[:, :, H:],
                                              ps_s[:, TJ * BPG * H:TJ * (BPG * H + E)].rearrange("p (j e) -> p j e", j=TJ),
                                              inv_alpha[:, 4:5], None, ALU.mult)
                link(ins, g)
                nc.vector.tensor_reduce(top[:, :, 0], logits[:, :, 0:H], AX.X, ALU.max)
                link(nc.vector.tensor_reduce(top[:, :, 1], logits[:, :, H:], AX.X, ALU.max), g)
                nc.vector.tensor_tensor(shifted[:, :, 0:H], logits[:, :, 0:H], top[:, :, 0:1].broadcast_to([P, TJ, H]), ALU.subtract)
                nc.vector.tensor_tensor(shifted[:, :, H:], logits[:, :, H:], top[:, :, 1:2].broadcast_to([P, TJ, E]),
                                        ALU.subtract).then_inc(shifted_ready, 1)

            def route(g):
                dve.wait_ge(exp_ready, after(g))
                nc.vector.tensor_reduce(sums[:, :, 0], expd[:, :, 0:H], AX.X, ALU.add)
                link(nc.vector.tensor_reduce(sums[:, :, 1], expd[:, :, H:], AX.X, ALU.add), g)
                link(nc.vector.reciprocal(sums_inv[:], sums[:]), g)
                link(nc.vector.tensor_tensor(score[:], expd[:, :, H:], sums_inv[:, :, 1:2].broadcast_to([P, TJ, E]), ALU.mult), g)
                link(nc.vector.tensor_tensor(diff[:], score[:].unsqueeze(2).broadcast_to([P, TJ, E, E]),
                                             score[:].unsqueeze(3).broadcast_to([P, TJ, E, E]), ALU.subtract), g)

                def flat(a):
                    return a.rearrange("p j e f -> p j (e f)")

                link(nc.vector.scalar_tensor_tensor(flat(tied[:]), flat(diff[:]), 0.0,
                                                    before[:].rearrange("p e f -> p (e f)").unsqueeze(1).broadcast_to([P, TJ, E * E]),
                                                    ALU.is_ge, ALU.mult), g)
                link(nc.vector.scalar_tensor_tensor(flat(ahead[:]), flat(diff[:]), 0.0, flat(tied[:]), ALU.is_gt, ALU.max), g)
                link(nc.vector.tensor_reduce(rank[:], ahead[:], AX.X, ALU.add), g)
                link(nc.vector.scalar_tensor_tensor(picked[:], rank[:], 1.5, score[:], ALU.is_lt, ALU.mult), g)
                link(nc.vector.tensor_reduce(picked_sum[:], picked[:], AX.X, ALU.add), g)
                link(nc.vector.tensor_scalar(picked_eps[:], picked_sum[:], TOPK_EPS, None, ALU.add), g)
                link(nc.vector.reciprocal(picked_inv[:], picked_eps[:]), g)
                nc.vector.scalar_tensor_tensor(combine[:], picked[:], ROUTED_SCALE,
                                               picked_inv[:].unsqueeze(2).broadcast_to([P, TJ, E]),
                                               ALU.mult, ALU.mult).then_inc(routed, 1)

            def attend(g):
                dve.wait_ge(pi_ready, after(g))
                for b in range(BPG):
                    ins = nc.vector.tensor_tensor_reduce(out=batch(weighted[:], b), in0=batch(w_sq[:], b), in1=batch(pi_bc[:], b),
                                                         scale=1.0, scalar=0.0, op0=ALU.mult, op1=ALU.add,
                                                         accum_out=dots[:, b:b + 1])
                link(ins, g)
                link(nc.vector.scalar_tensor_tensor(attn_den[:], pi_sum[:], PI_EPS, dots[:], ALU.add, ALU.add), g)
                link(nc.vector.reciprocal(attn_inv[:], attn_den[:]), g)
                link(nc.vector.scalar_tensor_tensor(attn[:], pi_sum[:], PI_EPS, attn_inv[:], ALU.add, ALU.mult), g)
                if not early(g, 2):
                    dve.wait_ge(down_done, count(shift(g, -2), NT, NT))
                for b in range(BPG):
                    ins = nc.vector.scalar_tensor_tensor(batch(attn_out[:, g[1] % 2], b), batch(ps_w[:], b), attn[:, b:b + 1],
                                                         batch(pi_bc[:], b), ALU.mult, ALU.mult)
                ins.then_inc(attn_ready, 1)

            def finish(g):
                dve.wait_ge(yT_ready, after(g))
                dve.wait_ge(x_res_loaded[g[1] % 2], loads(g))
                if not early(g, 2):
                    dve.wait_ge(stored[g[1] % 2], loads(shift(g, -2)))
                nc.vector.tensor_tensor(result[:, g[1] % 2], ps_w[:], x_res[:, g[1] % 2], ALU.add).then_inc(result_ready, 1)

            def rest_hidden(g, t):
                m = rows(t)
                dve.wait_ge(hid_hi_ready, count(g, NT, t + 1))
                if not (early(g, 1) and t < RING):
                    dve.wait_ge(down_done, count(g, NT, t + 1 - RING))
                r = (g[1] * NT + t) % RING
                nc.vector.tensor_tensor(hid_lo[0:m, r], hidden[0:m, r], hid_hi[0:m, r], ALU.subtract).then_inc(hid_lo_ready, 1)

            nc.vector.memset(down_raw[MLAST:P, WID - P:], 0.0)
            statistics((0, 0))
            statistics_written((0, 0))
            mean_variance()
            normalise((0, 0))
            rest_x((0, 0))
            dve.wait_ge(setup_transposed, 1)
            dve.wait_ge(small_loaded, 16 * 5)
            dve.wait_ge(consts_done, 1)
            nc.vector.tensor_copy(qkvT[:], ps_w[:, 0:P])
            nc.vector.tensor_copy(routerT[:], ps_w[:, 2 * P:2 * P + E])
            setup_link(nc.vector.tensor_tensor(head_sel[:], head_sel[:], temp_bc[:], ALU.mult))
            nc.vector.tensor_reduce(maxima[:, 3:4], qkvT[:], AX.X, ALU.max, apply_absolute_value=True)
            nc.vector.tensor_reduce(maxima[:, 4:5], routerT[:], AX.X, ALU.max, apply_absolute_value=True)
            dve.wait_ge(gate_loaded, 32)
            nc.vector.tensor_reduce(maxima[:, 0:1], gate_raw[:], AX.X, ALU.max, apply_absolute_value=True)
            dve.wait_ge(up_loaded, 32)
            nc.vector.tensor_reduce(maxima[:, 1:2], up_raw[:], AX.X, ALU.max, apply_absolute_value=True)
            dve.wait_ge(down_loaded, 48)
            nc.vector.tensor_reduce(maxima[:, 2:3], down_raw[:], AX.X, ALU.max, apply_absolute_value=True).then_inc(maxima_ready, 1)
            dve.wait_ge(maxima_spread, 1)
            setup_link(nc.vector.tensor_scalar(clamped[:], max_all[:], 2.0 ** -30, None, ALU.max))
            setup_link(nc.vector.tensor_scalar(power[:].bitcast(U32), clamped[:].bitcast(U32), EXP_MASK, None, ALU.bitwise_and))
            nc.vector.tensor_scalar(alpha[:].bitcast(U32), power[:].bitcast(U32), -1.0, over(14), ALU.mult, ALU.add)
            nc.vector.tensor_scalar(inv_alpha[:], power[:], 2.0 ** -14, None, ALU.mult)
            setup_link(nc.vector.tensor_scalar(gate_pow[:], power[:, 0:1], 2.0 ** -8, None, ALU.max))
            setup_link(nc.vector.tensor_scalar(beta[:].bitcast(U32), gate_pow[:].bitcast(U32), -1.0, over(-17), ALU.mult, ALU.add))
            setup_link(nc.vector.tensor_scalar(gamma[:], beta[:], alpha[:, 1:2], alpha[:, 2:3], ALU.mult, ALU.mult))
            setup_link(nc.vector.tensor_scalar(neg_gamma_q[:], gamma[:], inv_alpha[:, 3:4], -1.0, ALU.mult, ALU.mult))
            setup_link(nc.vector.tensor_scalar(gate_pow[:], gate_pow[:], inv_alpha[:, 1:2], inv_alpha[:, 2:3], ALU.mult, ALU.mult))
            setup_link(nc.vector.tensor_scalar(inv_gamma[:], gate_pow[:], 2.0 ** 17, None, ALU.mult))
            nc.vector.tensor_scalar(woutT[:], ps_w[:, P:2 * P], neg_gamma_q[:, 0:1], None, ALU.mult)
            nc.vector.tensor_scalar(qkv_hi[:], qkvT[:], alpha[:, 3:4], None, ALU.mult)
            setup_link(nc.vector.tensor_scalar(router_hi[:], routerT[:], alpha[:, 4:5], None, ALU.mult))
            nc.vector.scalar_tensor_tensor(qkv_lo[:], qkvT[:], alpha[:, 3:4], qkv_hi[:], ALU.mult, ALU.subtract)
            nc.vector.scalar_tensor_tensor(router_lo[:], routerT[:], alpha[:, 4:5], router_hi[:], ALU.mult,
                                           ALU.subtract).then_inc(scales_ready, 1)
            cols = E * F
            for i, (raw, hi, lo) in enumerate(((gate_raw, gate_hi, gate_lo), (up_raw, up_hi, up_lo))):
                dve.wait_ge(weights_hi, i + 1)
                nc.vector.scalar_tensor_tensor(lo[:, 0:cols].rearrange("d (k p) -> d k p", k=KE),
                                               raw[:, 0:cols].rearrange("d (p k) -> d k p", k=KE), alpha[:, i:i + 1],
                                               hi[:, 0:cols].rearrange("d (k p) -> d k p", k=KE), ALU.mult, ALU.subtract)
                nc.vector.scalar_tensor_tensor(lo[:, cols:cols + FS], raw[:, cols:], alpha[:, i:i + 1],
                                               hi[:, cols:cols + FS], ALU.mult, ALU.subtract).then_inc(weights_ready, 1)
            dve.wait_ge(weights_hi, 3)
            nc.vector.scalar_tensor_tensor(down_lo[:], down_raw[:], alpha[:, 2:3], down_hi[:], ALU.mult,
                                           ALU.subtract).then_inc(weights_ready, 1)
            head_scales((0, 0))
            shift_logits((0, 0))
            route((0, 0))
            attend((0, 0))

            def body(g, more):
                for t in range(NT):
                    n = g[1] * NT + t
                    m = rows(t)
                    if t == 1 and more:
                        statistics_written(shift(g, 1))
                    if t < KE:
                        dve.wait_ge(combined, count(g, KE, t + 1))
                    else:
                        dve.wait_ge(silu_ready, count(g, NT, t + 1))
                    dve.wait_ge(up_ready, count(g, NT, t + 1))
                    if not (early(g, 1) and t < RING):
                        dve.wait_ge(hid_hi_ready, count(g, NT, t + 1 - RING))
                    nc.vector.scalar_tensor_tensor(hidden[0:m, n % RING], act_gate[0:m, n % RING], beta[0:m, 0:1],
                                                   ps_up[0:m, n % 2], ALU.mult, ALU.mult).then_inc(hid_ready, 1)
                    if t >= 1:
                        rest_hidden(g, t - 1)
                    elif not early(g, 1):
                        rest_hidden(shift(g, -1), NT - 1)
                    if t == 4 and not early(g, 1):
                        finish(shift(g, -1))
                    if more:
                        if t == 0:
                            statistics(shift(g, 1))
                        if t == 1:
                            mean_variance()
                        if t == 2:
                            normalise(shift(g, 1))
                        if t == 4:
                            rest_x(shift(g, 1))
                        if t == 6:
                            head_scales(shift(g, 1))
                        if t == 8:
                            shift_logits(shift(g, 1))
                        if t == 9:
                            route(shift(g, 1))
                        if t == 13:
                            attend(shift(g, 1))
                            assert step[0] == dve_per_group, step[0]

            run(dve, (0, 0), body)
            rest_hidden((0, G - 1), NT - 1)
            finish((0, G - 1))

        @block.tensor
        def _(pe):
            def three(out_ap, hi, lo, m_hi, m_lo, start, stop):
                nc.tensor.matmul(out_ap, hi, m_hi, start=start, stop=False)
                nc.tensor.matmul(out_ap, hi, m_lo, start=False, stop=False)
                return nc.tensor.matmul(out_ap, lo, m_hi, start=False, stop=stop)

            def transpose_x(g):
                pe.wait_ge(xn_ready, after(g))
                if not early(g, 1):
                    pe.wait_ge(pi_ready, after(g, 0))
                for j in range(TJ):
                    ins = nc.tensor.transpose(ps_x[:, j * P:(j + 1) * P], xn[:, j], ident[:])
                ins.then_inc(xT_ready, 1)

            def project_w(g):
                q = g[1] % 2
                pe.wait_ge(lo_x_ready, after(g))
                if not early(g, 1):
                    pe.wait_ge(combine_ready, after(g, 0))
                if not early(g, 2):
                    pe.wait_ge(result_ready, after(shift(g, -1), 0))
                at = TJ * BPG * H
                for j in range(TJ):
                    c = slice(j * P, (j + 1) * P)
                    o = ps_s[:, at + j * E:at + (j + 1) * E]
                    nc.tensor.matmul(o, xT_hi[:, q, c], router_hi[:], start=True, stop=False)
                    nc.tensor.matmul(o, xT_hi[:, q, c], router_lo[:], start=False, stop=False)
                    nc.tensor.matmul(o, xT_lo[:, q, c], router_hi[:], start=False, stop=True)
                three(ps_w[:], qkv_hi[:], qkv_lo[:], xT_hi[:, q], xT_lo[:, q], True, True).then_inc(w_ready, 1)

            def head_logits(g):
                pe.wait_ge(head_scaled_ready, after(g))
                for j in range(TJ):
                    w = BPG * H
                    ins = nc.tensor.matmul(ps_s[:, j * w:(j + 1) * w], w_sq[:, j * P:(j + 1) * P],
                                           head_scaled[:].rearrange("p b h -> p (b h)"), start=True, stop=True)
                ins.then_inc(logits_ready, 1)

            def spread(g):
                pe.wait_ge(wide_ready, after(g))
                for j in range(TJ):
                    c = slice(j * P, (j + 1) * P)
                    nc.tensor.transpose(ps_x[:, c], pi_wide[:, j].rearrange("p h d -> p (h d)"), ident[:])
                    ins = nc.tensor.transpose(ps_s[:, c], combine_wide[:, j].rearrange("p e f -> p (e f)"), ident[:])
                ins.then_inc(spread_ready, 1)

            def down(g, t):
                m = rows(t)
                r = (g[1] * NT + t) % RING
                c = slice(t * P, (t + 1) * P)
                pe.wait_ge(hid_lo_ready, count(g, NT, t + 1))
                if t == 0 and not early(g, 1):
                    pe.wait_ge(y_taken, after(g, 0))
                if t == NT - 2:
                    pe.wait_ge(attn_ready, after(g))
                    nc.tensor.matmul(ps_y[:], woutT[:], attn_out[:, g[1] % 2], start=False, stop=False)
                three(ps_y[:], down_hi[0:m, c], down_lo[0:m, c], hid_hi[0:m, r], hid_lo[0:m, r],
                      t == 0, t == NT - 1).then_inc(down_done, 1)

            def transpose_y(g):
                pe.wait_ge(y_taken, after(g))
                if not (fixed(g) and g[1] == G - 1):
                    pe.wait_ge(attn_ready, after(shift(g, 1)))
                for j in range(TJ):
                    ins = nc.tensor.transpose(ps_w[:, j * P:(j + 1) * P], yT[:, j * P:(j + 1) * P], ident[:])
                ins.then_inc(yT_ready, 1)

            pe.wait_ge(consts_done, 1)
            transpose_x((0, 0))
            pe.wait_ge(small_loaded, 16 * 5)
            nc.tensor.transpose(ps_w[:, 0:P], qkv_raw[:], ident[:])
            nc.tensor.transpose(ps_w[:, P:2 * P], out_raw[:], ident[:])
            nc.tensor.transpose(ps_w[:, 2 * P:2 * P + E], router_raw[:], ident[0:E, 0:E]).then_inc(setup_transposed, 1)
            pe.wait_ge(scales_ready, 1)
            project_w((0, 0))
            head_logits((0, 0))
            spread((0, 0))
            pe.wait_ge(weights_ready, 3)

            def body(g, more):
                q = g[1] % 2
                for t in range(NT):
                    n = g[1] * NT + t
                    c = slice(t * P, t * P + rows(t))
                    m = rows(t)
                    if not (early(g, 1) and t < 2):
                        pe.wait_ge(silu_ready, count(g, NT, t - 1))
                    three(ps_gate[0:m, n % 2], gate_hi[:, c], gate_lo[:, c], xT_hi[:, q], xT_lo[:, q],
                          True, True).then_inc(gate_ready, 1)
                    if not (early(g, 1) and t < 2):
                        pe.wait_ge(hid_ready, count(g, NT, t - 1))
                    three(ps_up[0:m, n % 2], up_hi[:, c], up_lo[:, c], xT_hi[:, q], xT_lo[:, q],
                          True, True).then_inc(up_ready, 1)
                    if t >= LAG:
                        down(g, t - LAG)
                    elif not early(g, 1):
                        down(shift(g, -1), t + NT - LAG)
                    if t == LAG and not early(g, 1):
                        transpose_y(shift(g, -1))
                    if more:
                        if t == 3:
                            transpose_x(shift(g, 1))
                        if t == 5:
                            project_w(shift(g, 1))
                        if t == 7:
                            head_logits(shift(g, 1))
                        if t == 11:
                            spread(shift(g, 1))

            run(pe, (0, 0), body)
            for t in range(NT - LAG, NT):
                down((0, G - 1), t)
            transpose_y((0, G - 1))


_INS = ['L0_attn_x', 'L0_attn_Wqkv', 'L0_attn_temp', 'L0_attn_Wout', 'L0_attn_bout', 'L0_ffn_gate_w', 'L0_ffn_w_gate',
        'L0_ffn_w_up', 'L0_ffn_w_down', 'L0_ffn_sw_gate', 'L0_ffn_sw_up', 'L0_ffn_sw_down']


def kernel(**inputs):
    import numpy as np
    import concourse.bacc as bacc
    from concourse.bass_utils import run_bass_kernel_spmd

    nc = bacc.Bacc("TRN2", target_bir_lowering=False, num_devices=1)
    arrays, args = {}, []
    for name in _INS:
        a = np.ascontiguousarray(inputs[name])
        arrays[f"in_{name}"] = a
        args.append(nc.dram_tensor(f"in_{name}", a.shape, mybir.dt.from_np(a.dtype), kind="ExternalInput").ap())
    out = nc.dram_tensor("out", arrays["in_L0_attn_x"].shape, F32, kind="ExternalOutput").ap()
    attn_moe_kernel(nc, *args, out)
    r = run_bass_kernel_spmd(nc, [arrays], core_ids=[0])
    return r.results[0]["out"]
```

```python
from contextlib import ExitStack

import concourse.bass as bass
from concourse import mybir

ALU = mybir.AluOpType
ACT = mybir.ActivationFunctionType
AX = mybir.AxisListType
F32 = mybir.dt.float32
F16 = mybir.dt.float16
U32 = mybir.dt.uint32

P = 128
BLK = 512
TJ = BLK // P
LN_EPS = 1e-5
NORM_EPS_SQ = 1e-12 ** 2
PI_EPS = 1e-8
TOPK_EPS = 1e-20
ROUTED_SCALE = 2.5
LAG = 6
RING = 4
SPLIT_RING = 7
POOL_REST = (5, 11, 12, 13)

EXP_MASK = 0x7F800000


def over(k):
    return float((254 + k) << 23)


def attn_moe_kernel(nc, x, Wqkv, temp, Wout, bout, gate_w, w_gate, w_up, w_down, sw_gate, sw_up, sw_down, out):
    NB, N, D = x.shape
    E, _, F = w_gate.shape
    FS = sw_gate.shape[1]
    H = temp.shape[0]
    HD = D // H
    G = NB * N // BLK
    BPG = BLK // N
    ROWS = N // TJ
    KE = F * E // P
    ER = P // E
    NT = KE + -(-FS // P)
    MLAST = FS - (NT - 1 - KE) * P
    assert D == P and F == ER * KE and BPG * ROWS == P and G % 2 == 0 and G >= 6 and NT % 2 == 0 and NT % SPLIT_RING == 0 and 2 * NT % RING == 0 and BPG == 2
    WID = NT * P

    x_view = x.rearrange("b n d -> (b n) d").rearrange("(g p j) d -> g p (j d)", p=P, j=TJ)
    out_view = out.rearrange("b n d -> (b n) d").rearrange("(g p j) d -> g p (j d)", p=P, j=TJ)

    with ExitStack() as ctx:
        def sb(name, shape, dt=F32):
            return ctx.enter_context(nc.sbuf_tensor(name, shape, dt))

        def ps(name, shape, dt=F32):
            return ctx.enter_context(nc.psum_tensor(name, shape, dt))

        def sem(name):
            return ctx.enter_context(nc.semaphore(name))

        gate_raw = sb("gate_raw", [P, E * F + FS])
        up_raw = sb("up_raw", [P, E * F + FS])
        down_raw = sb("down_raw", [P, WID])
        qkv_raw = sb("qkv_raw", [P, P])
        out_raw = sb("out_raw", [P, P])
        router_raw = sb("router_raw", [E, P])
        gate_hi = sb("gate_hi", [P, WID], F16)
        gate_lo = sb("gate_lo", [P, WID], F16)
        up_hi = sb("up_hi", [P, WID], F16)
        up_lo = sb("up_lo", [P, WID], F16)
        down_hi = sb("down_hi", [P, WID], F16)
        down_lo = sb("down_lo", [P, WID], F16)
        qkv_hi = sb("qkv_hi", [P, P], F16)
        qkv_lo = sb("qkv_lo", [P, P], F16)
        router_hi = sb("router_hi", [P, E], F16)
        router_lo = sb("router_lo", [P, E], F16)
        qkvT = sb("qkvT", [P, P])
        routerT = sb("routerT", [P, E])
        woutT = sb("woutT", [P, P])
        temp_bc = sb("temp_bc", [P, H])
        bias_col = sb("bias_col", [P, 1])

        ident = sb("ident", [P, P])
        head_sel = sb("head_sel", [P, H])
        before = sb("before", [P, E, E])
        neg_half = sb("neg_half", [P, TJ])
        ln_eps = sb("ln_eps", [P, TJ])
        maxima = sb("maxima", [P, 5])
        max_all = sb("max_all", [P, 5])
        clamped = sb("clamped", [P, 5])
        power = sb("power", [P, 5])
        alpha = sb("alpha", [P, 5])
        inv_alpha = sb("inv_alpha", [P, 5])
        gate_pow = sb("gate_pow", [P, 1])
        beta = sb("beta", [P, 1])
        gamma = sb("gamma", [P, 1])
        inv_gamma = sb("inv_gamma", [P, 1])
        neg_gamma_q = sb("neg_gamma_q", [P, 1])

        x_in = sb("x_in", [P, 2, TJ, P])
        x_res = sb("x_res", [P, 2, BLK])
        stats = sb("stats", [P, TJ, 6])
        mean_var = sb("mean_var", [P, TJ, 2])
        var_eps = sb("var_eps", [P, TJ])
        rstd = sb("rstd", [P, TJ])
        xn = sb("xn", [P, TJ, P])
        xT_hi = sb("xT_hi", [P, 2, BLK], F16)
        xT_lo = sb("xT_lo", [P, 2, BLK], F16)
        w_sq = sb("w_sq", [P, BLK])
        norm_sq = sb("norm_sq", [P, BPG])
        norm_max = sb("norm_max", [P, BPG])
        norm_inv = sb("norm_inv", [P, BPG])
        head_scaled = sb("head_scaled", [P, BPG, H])
        logits = sb("logits", [P, TJ, H + E])
        top = sb("top", [P, TJ, 2])
        shifted = sb("shifted", [P, TJ, H + E])
        expd = sb("expd", [P, TJ, H + E])
        sums = sb("sums", [P, TJ, 2])
        sums_inv = sb("sums_inv", [P, TJ, 2])
        score = sb("score", [P, TJ, E])
        diff = sb("diff", [P, TJ, E, E])
        tied = sb("tied", [P, TJ, E, E])
        outscored = sb("outscored", [P, TJ, E, E])
        rank = sb("rank", [P, TJ, E])
        picked = sb("picked", [P, TJ, E])
        picked_sum = sb("picked_sum", [P, TJ])
        picked_eps = sb("picked_eps", [P, TJ])
        picked_inv = sb("picked_inv", [P, TJ])
        combine_scale = sb("combine_scale", [P, TJ])
        pi_wide = sb("pi_wide", [P, TJ, H, HD])
        combine_wide = sb("combine_wide", [P, TJ, E, ER])
        pi_bc = sb("pi_bc", [P, BLK])
        pi_sum = sb("pi_sum", [P, BPG])
        weighted = sb("weighted", [P, BLK])
        dots = sb("dots", [P, BPG])
        attn_den = sb("attn_den", [P, BPG])
        attn_inv = sb("attn_inv", [P, BPG])
        attn = sb("attn", [P, BPG])
        attn_out = sb("attn_out", [P, 2, BLK])
        combine_bc = sb("combine_bc", [P, 2, BLK])

        act_gate = sb("act_gate", [P, RING, BLK])
        hidden = sb("hidden", [P, RING, BLK])
        hid_hi = sb("hid_hi", [P, SPLIT_RING, BLK], F16)
        hid_lo = sb("hid_lo", [P, SPLIT_RING, BLK], F16)
        yT = sb("yT", [P, BLK])
        result = sb("result", [P, 2, BLK])

        ps_gate = ps("ps_gate", [P, 2, BLK])
        ps_up = ps("ps_up", [P, 2, BLK])
        ps_y = ps("ps_y", [P, BLK])
        ps_x = ps("ps_x", [P, BLK])
        ps_w = ps("ps_w", [P, BLK])
        ps_s = ps("ps_s", [P, BLK])

        x_in_loaded = [sem("x_in_loaded0"), sem("x_in_loaded1")]
        x_res_loaded = [sem("x_res_loaded0"), sem("x_res_loaded1")]
        stored = [sem("stored0"), sem("stored1")]
        small_loaded = sem("small_loaded")
        gate_loaded, up_loaded, down_loaded = sem("gate_loaded"), sem("up_loaded"), sem("down_loaded")
        consts_step, consts_done = sem("consts_step"), sem("consts_done")
        setup_transposed = sem("setup_transposed")
        setup_step = sem("setup_step")
        maxima_ready, maxima_spread = sem("maxima_ready"), sem("maxima_spread")
        scales_ready, weights_hi, weights_ready = sem("scales_ready"), sem("weights_hi"), sem("weights_ready")
        stats_written = sem("stats_written")
        dve_step = sem("dve_step")
        pool_step = sem("pool_step")
        stats_ready, rstd_ready, xn_ready = sem("stats_ready"), sem("rstd_ready"), sem("xn_ready")
        xT_ready, hi_x_ready, lo_x_ready = sem("xT_ready"), sem("hi_x_ready"), sem("lo_x_ready")
        w_ready, wsq_ready, head_scaled_ready = sem("w_ready"), sem("wsq_ready"), sem("head_scaled_ready")
        logits_ready, shifted_ready, exp_ready = sem("logits_ready"), sem("shifted_ready"), sem("exp_ready")
        routed, wide_ready, spread_ready = sem("routed"), sem("wide_ready"), sem("spread_ready")
        pi_ready, combine_ready, attn_ready = sem("pi_ready"), sem("combine_ready"), sem("attn_ready")
        gate_ready, up_ready, silu_ready = sem("gate_ready"), sem("up_ready"), sem("silu_ready")
        combined, hid_ready = sem("combined"), sem("hid_ready")
        hid_hi_ready, down_done = sem("hid_hi_ready"), sem("down_done")
        hid_lo_ready, pool_lo_ready = sem("hid_lo_ready"), sem("pool_lo_ready")
        y_taken, yT_ready, result_ready = sem("y_taken"), sem("yT_ready"), sem("result_ready")

        def count(g, per, k):
            m, c = g
            return m * (2 * per) + (c * per + k)

        def after(g, k=1):
            return count(g, 1, k)

        def loads(g):
            m, c = g
            return m * 16 + 16 * (c // 2 + 1)

        def shift(g, by):
            return (g[0], g[1] + by)

        def fixed(g):
            return isinstance(g[0], int)

        def early(g, n):
            return fixed(g) and 2 * g[0] + g[1] < n

        def batch(ap, b):
            return ap.rearrange("p (j b q) -> p b j q", j=TJ, b=BPG)[:, b]

        def weighed(eng, g, t):
            if t < KE:
                eng.wait_ge(combined, count(g, KE, t + 1))
            else:
                eng.wait_ge(hid_ready, count(g, NT, t + 1))

        def rest_taken(eng, g, t, by=None):
            if t in POOL_REST:
                eng.wait_ge(pool_lo_ready, count(g, len(POOL_REST), 1 + POOL_REST.index(t)))
            else:
                eng.wait_ge(hid_lo_ready, count(g, NT - len(POOL_REST), 1 + sum(u not in POOL_REST for u in range(t))))

        def back(g, t, by):
            return (g, t - by) if t >= by else (shift(g, -1), t - by + NT)

        def rows(t):
            return MLAST if t == NT - 1 else P

        def rows_of(g):
            return x_view[g[0] * 2 + g[1]], out_view[g[0] * 2 + g[1]]

        def run(eng, body):
            body((0, 0))
            with eng.Fori(0, (G - 4) // 2) as m:
                body((m, 1))
                body((m, 2))
            for c in range(G - 3, G):
                body((0, c))

        def ahead_of(g, by):
            return not fixed(g) or g[1] + by < G

        block = ctx.enter_context(nc.Block())

        @block.sync
        def _(sp):
            def load_x_in(g):
                if not early(g, 2):
                    sp.wait_ge(xn_ready, after(shift(g, -2)))
                sp.dma_start(x_in[:, g[1] % 2].rearrange("p j d -> p (j d)"), rows_of(g)[0]).then_inc(x_in_loaded[g[1] % 2], 16)

            def load_x_res(g):
                if not early(g, 2):
                    sp.wait_ge(result_ready, after(shift(g, -2)))
                sp.dma_start(x_res[:, g[1] % 2], rows_of(g)[0]).then_inc(x_res_loaded[g[1] % 2], 16)

            def store(g):
                sp.wait_ge(result_ready, after(g))
                sp.dma_start(rows_of(g)[1], result[:, g[1] % 2]).then_inc(stored[g[1] % 2], 16)

            load_x_in((0, 0))
            sp.dma_start(gate_raw[:, 0:E * F].rearrange("d (e f) -> d e f", e=E),
                         w_gate.rearrange("e d f -> d e f")).then_inc(gate_loaded, 16)
            sp.dma_start(gate_raw[:, E * F:], sw_gate).then_inc(gate_loaded, 16)
            sp.dma_start(down_raw[:, 0:KE * P], w_down.rearrange("e f d -> (e f) d").rearrange("(p k) d -> p (k d)", k=KE)).then_inc(down_loaded, 16)
            full = FS - MLAST
            sp.dma_start(down_raw[:, KE * P:WID - P].rearrange("p (k d) -> p k d", d=P),
                         sw_down[0:full, :].rearrange("(k p) d -> p k d", p=P)).then_inc(down_loaded, 16)
            sp.dma_start(down_raw[0:MLAST, WID - P:], sw_down[full:, :]).then_inc(down_loaded, 16)
            load_x_in((0, 1))
            load_x_in((0, 2))
            load_x_res((0, 0))

            def body(g):
                if ahead_of(g, 3):
                    load_x_in(shift(g, 3))
                if ahead_of(g, 1):
                    load_x_res(shift(g, 1))
                if not early(g, 1):
                    store(shift(g, -1))

            run(sp, body)
            store((0, G - 1))
            for half in stored:
                sp.wait_ge(half, 16 * (G // 2))

        @block.gpsimd
        def _(pool):
            nc.gpsimd.memset(ident[:], 0.0).then_inc(consts_step, 1)
            nc.gpsimd.memset(head_sel[:], 1.0).then_inc(consts_step, 1)
            nc.gpsimd.memset(before[:], 1.0).then_inc(consts_step, 1)
            nc.gpsimd.memset(neg_half[:], -0.5).then_inc(consts_step, 1)
            nc.gpsimd.memset(ln_eps[:], LN_EPS).then_inc(consts_step, 1)
            pool.wait_ge(consts_step, 3)
            nc.gpsimd.affine_select(out=ident[:], in_=ident[:], compare_op=ALU.not_equal, fill=1.0, base=0,
                                    pattern=[[-1, P]], channel_multiplier=1).then_inc(consts_step, 1)
            nc.gpsimd.affine_select(out=before[:], in_=before[:], compare_op=ALU.is_gt, fill=0.0, base=0,
                                    pattern=[[1, E], [-1, E]], channel_multiplier=0).then_inc(consts_step, 1)
            nc.gpsimd.affine_select(out=head_sel[:], in_=head_sel[:], compare_op=ALU.is_ge, fill=0.0, base=0,
                                    pattern=[[-HD, H]], channel_multiplier=1).then_inc(consts_step, 1)
            pool.wait_ge(consts_step, 8)
            nc.gpsimd.affine_select(out=head_sel[:], in_=head_sel[:], compare_op=ALU.is_gt, fill=0.0, base=HD,
                                    pattern=[[HD, H]], channel_multiplier=-1).then_inc(consts_done, 1)

            def layer_norm(g):
                pool.wait_ge(stats_ready, after(g))
                nc.gpsimd.tensor_tensor(var_eps[:], mean_var[:, :, 1], ln_eps[:], ALU.add).then_inc(pool_step, 1)
                pool.wait_ge(pool_step, after(g))
                nc.gpsimd.tensor_tensor(rstd[:], var_eps[:], neg_half[:], ALU.pow).then_inc(rstd_ready, 1)

            def widen(g):
                pool.wait_ge(routed, after(g))
                nc.gpsimd.tensor_tensor(pi_wide[:], expd[:, :, 0:H].unsqueeze(3).broadcast_to([P, TJ, H, HD]),
                                        sums_inv[:, :, 0:1].unsqueeze(3).broadcast_to([P, TJ, H, HD]), ALU.mult)
                nc.gpsimd.tensor_tensor(combine_wide[:], picked[:].unsqueeze(3).broadcast_to([P, TJ, E, ER]),
                                        combine_scale[:].unsqueeze(2).unsqueeze(3).broadcast_to([P, TJ, E, ER]), ALU.mult).then_inc(wide_ready, 1)

            layer_norm((0, 0))
            pool.wait_ge(maxima_ready, 1)
            nc.gpsimd.partition_all_reduce(max_all[:], maxima[:], P, bass.bass_isa.ReduceOp.max).then_inc(maxima_spread, 1)
            widen((0, 0))
            layer_norm((0, 1))

            def rest_hidden(g, t):
                m, r = rows(t), t % SPLIT_RING
                pool.wait_ge(hid_hi_ready, count(g, NT, t + 1))
                if not (early(g, 1) and t < SPLIT_RING):
                    pool.wait_ge(down_done, count(g, NT, t + 1 - SPLIT_RING))
                nc.gpsimd.tensor_tensor(hid_lo[0:m, r], hidden[0:m, (g[1] * NT + t) % RING], hid_hi[0:m, r],
                                        ALU.subtract).then_inc(pool_lo_ready, 1)

            def body(g):
                for t in range(NT):
                    if t < KE:
                        pool.wait_ge(hid_ready, count(g, NT, t + 1))
                        if t == 0:
                            pool.wait_ge(combine_ready, after(g))
                        h = hidden[:, (g[1] * NT + t) % RING]
                        nc.gpsimd.tensor_tensor(h, h, combine_bc[:, g[1] % 2], ALU.mult).then_inc(combined, 1)
                    before_g, before_t = back(g, t, 1)
                    if before_t in POOL_REST and not (early(g, 1) and t == 0):
                        rest_hidden(before_g, before_t)
                    if t == 6 and ahead_of(g, 2):
                        layer_norm(shift(g, 2))
                    if t == 8 and ahead_of(g, 1):
                        widen(shift(g, 1))

            run(pool, body)
            rest_hidden((0, G - 1), NT - 1)

        @block.scalar
        def _(act):
            act.dma_start(qkv_raw[:], Wqkv).then_inc(small_loaded, 16)
            act.dma_start(out_raw[:], Wout).then_inc(small_loaded, 16)
            act.dma_start(router_raw[:], gate_w).then_inc(small_loaded, 16)
            act.dma_start(temp_bc[:], temp.rearrange("h o -> o h").broadcast_to([P, H])).then_inc(small_loaded, 16)
            act.dma_start(bias_col[:], bout.rearrange("(d o) -> d o", o=1)).then_inc(small_loaded, 16)
            act.dma_start(up_raw[:, 0:E * F].rearrange("d (e f) -> d e f", e=E),
                          w_up.rearrange("e d f -> d e f")).then_inc(up_loaded, 16)
            act.dma_start(up_raw[:, E * F:], sw_up).then_inc(up_loaded, 16)

            def split_x(g):
                act.wait_ge(xT_ready, after(g))
                nc.scalar.activation(xT_hi[:, g[1] % 2], ps_x[:], ACT.Copy).then_inc(hi_x_ready, 1)

            def square_w(g):
                act.wait_ge(w_ready, after(g))
                for b in range(BPG):
                    ins = nc.scalar.activation(batch(w_sq[:], b), batch(ps_w[:], b), ACT.Square,
                                               scale=inv_alpha[:, 3:4], accum_out=norm_sq[:, b:b + 1])
                ins.then_inc(wsq_ready, 1)

            def exponentials(g):
                act.wait_ge(shifted_ready, after(g))
                nc.scalar.activation(expd[:], shifted[:], ACT.Exp).then_inc(exp_ready, 1)

            def take_spread(g):
                act.wait_ge(spread_ready, after(g))
                for b in range(BPG):
                    ins = nc.scalar.activation(batch(pi_bc[:], b), batch(ps_x[:], b), ACT.Copy,
                                               accum_out=pi_sum[:, b:b + 1])
                ins.then_inc(pi_ready, 1)
                nc.scalar.activation(combine_bc[:, g[1] % 2], ps_s[:], ACT.Copy).then_inc(combine_ready, 1)

            def take_y(g):
                act.wait_ge(down_done, count(g, NT, NT))
                if not early(g, 1):
                    act.wait_ge(yT_ready, after(g, 0))
                nc.scalar.activation(yT[:], ps_y[:], ACT.Identity, bias=bias_col[:, 0:1],
                                     scale=inv_gamma[:, 0:1]).then_inc(y_taken, 1)

            def split_hidden(g, t):
                m = rows(t)
                weighed(act, g, t)
                if not (early(g, 1) and t < SPLIT_RING):
                    act.wait_ge(down_done, count(g, NT, t + 1 - SPLIT_RING))
                nc.scalar.activation(hid_hi[0:m, t % SPLIT_RING], hidden[0:m, (g[1] * NT + t) % RING], ACT.Copy).then_inc(hid_hi_ready, 1)

            split_x((0, 0))
            act.wait_ge(scales_ready, 1)
            cols = E * F
            act.wait_ge(gate_loaded, 32)
            nc.scalar.activation(gate_hi[:, 0:cols].rearrange("d (k p) -> d k p", k=KE),
                                 gate_raw[:, 0:cols].rearrange("d (p k) -> d k p", k=KE), ACT.Copy, scale=alpha[:, 0:1])
            nc.scalar.activation(gate_hi[:, cols:cols + FS], gate_raw[:, cols:], ACT.Copy, scale=alpha[:, 0:1]).then_inc(weights_hi, 1)
            act.wait_ge(up_loaded, 32)
            nc.scalar.activation(up_hi[:, 0:cols].rearrange("d (k p) -> d k p", k=KE),
                                 up_raw[:, 0:cols].rearrange("d (p k) -> d k p", k=KE), ACT.Copy, scale=alpha[:, 1:2])
            nc.scalar.activation(up_hi[:, cols:cols + FS], up_raw[:, cols:], ACT.Copy, scale=alpha[:, 1:2]).then_inc(weights_hi, 1)
            act.wait_ge(down_loaded, 48)
            nc.scalar.activation(down_hi[:], down_raw[:], ACT.Copy, scale=alpha[:, 2:3]).then_inc(weights_hi, 1)
            square_w((0, 0))
            exponentials((0, 0))
            take_spread((0, 0))

            def body(g):
                for t in range(NT):
                    if t == LAG and not early(g, 1):
                        take_y(shift(g, -1))
                    if ahead_of(g, 1):
                        if t == 3:
                            square_w(shift(g, 1))
                        if t == 7:
                            exponentials(shift(g, 1))
                        if t == 12:
                            take_spread(shift(g, 1))
                    act.wait_ge(gate_ready, count(g, NT, t + 1))
                    if not (early(g, 1) and t < RING):
                        act.wait_ge(hid_ready, count(g, NT, t + 1 - RING))
                    n = g[1] * NT + t
                    m = rows(t)
                    nc.scalar.activation(act_gate[0:m, n % RING], ps_gate[0:m, n % 2], ACT.Silu,
                                         scale=inv_alpha[0:m, 0:1]).then_inc(silu_ready, 1)
                    if t == 0 and ahead_of(g, 1):
                        if not early(g, 1):
                            act.wait_ge(up_ready, count(g, NT, 0))
                        split_x(shift(g, 1))
                    if not (early(g, 1) and t < 2):
                        split_hidden(*back(g, t, 2))

            run(act, body)
            split_hidden((0, G - 1), NT - 2)
            split_hidden((0, G - 1), NT - 1)
            take_y((0, G - 1))

        @block.vector
        def _(dve):
            dve_per_group = 19
            step = [0]

            def link(ins, g):
                step[0] += 1
                ins.then_inc(dve_step, 1)
                dve.wait_ge(dve_step, count(g, dve_per_group, step[0]))

            set_up = [0]

            def setup_link(ins):
                set_up[0] += 1
                ins.then_inc(setup_step, 1)
                dve.wait_ge(setup_step, set_up[0])

            def statistics(g):
                dve.wait_ge(x_in_loaded[g[1] % 2], loads(g))
                for j in range(TJ):
                    ins = nc.vector.bn_stats(stats[:, j], x_in[:, g[1] % 2, j])
                ins.then_inc(stats_written, 1)

            def statistics_written(g):
                dve.wait_ge(stats_written, after(g))

            def mean_variance():
                for j in range(TJ):
                    ins = nc.vector.bn_aggr(mean_var[:, j], stats[:, j])
                ins.then_inc(stats_ready, 1)

            def normalise(g):
                dve.wait_ge(rstd_ready, after(g))
                for j in range(TJ):
                    ins = nc.vector.tensor_scalar(xn[:, j], x_in[:, g[1] % 2, j], mean_var[:, j, 0:1], rstd[:, j:j + 1],
                                                  ALU.subtract, ALU.mult)
                ins.then_inc(xn_ready, 1)

            def rest_x(g):
                dve.wait_ge(hi_x_ready, after(g))
                nc.vector.tensor_tensor(xT_lo[:, g[1] % 2], ps_x[:], xT_hi[:, g[1] % 2], ALU.subtract).then_inc(lo_x_ready, 1)

            def head_scales(g):
                step[0] = 0
                dve.wait_ge(wsq_ready, after(g))
                link(nc.vector.tensor_scalar(norm_max[:], norm_sq[:], NORM_EPS_SQ, None, ALU.max), g)
                link(nc.vector.reciprocal(norm_inv[:], norm_max[:]), g)
                for b in range(BPG):
                    ins = nc.vector.tensor_scalar(head_scaled[:, b], head_sel[:], norm_inv[:, b:b + 1], None, ALU.mult)
                ins.then_inc(head_scaled_ready, 1)

            def shift_logits(g):
                dve.wait_ge(logits_ready, after(g))
                raw = ps_s[:, 0:TJ * BPG * H].rearrange("p (j b h) -> p j b h", j=TJ, b=BPG)
                for b in range(BPG):
                    r = slice(b * ROWS, (b + 1) * ROWS)
                    nc.vector.tensor_copy(logits[r, :, 0:H], raw[r, :, b])
                ins = nc.vector.tensor_scalar(logits[:, :, H:],
                                              ps_s[:, TJ * BPG * H:TJ * (BPG * H + E)].rearrange("p (j e) -> p j e", j=TJ),
                                              inv_alpha[:, 4:5], None, ALU.mult)
                link(ins, g)
                nc.vector.tensor_reduce(top[:, :, 0], logits[:, :, 0:H], AX.X, ALU.max)
                link(nc.vector.tensor_reduce(top[:, :, 1], logits[:, :, H:], AX.X, ALU.max), g)
                nc.vector.tensor_tensor(shifted[:, :, 0:H], logits[:, :, 0:H], top[:, :, 0:1].broadcast_to([P, TJ, H]), ALU.subtract)
                nc.vector.tensor_tensor(shifted[:, :, H:], logits[:, :, H:], top[:, :, 1:2].broadcast_to([P, TJ, E]),
                                        ALU.subtract).then_inc(shifted_ready, 1)

            def rank_experts(g):
                dve.wait_ge(exp_ready, after(g))
                nc.vector.tensor_reduce(sums[:, :, 0], expd[:, :, 0:H], AX.X, ALU.add)
                link(nc.vector.tensor_reduce(sums[:, :, 1], expd[:, :, H:], AX.X, ALU.add), g)
                link(nc.vector.reciprocal(sums_inv[:], sums[:]), g)
                link(nc.vector.tensor_tensor(score[:], expd[:, :, H:], sums_inv[:, :, 1:2].broadcast_to([P, TJ, E]), ALU.mult), g)
                link(nc.vector.tensor_tensor(diff[:], score[:].unsqueeze(2).broadcast_to([P, TJ, E, E]),
                                             score[:].unsqueeze(3).broadcast_to([P, TJ, E, E]), ALU.subtract), g)

                def flat(a):
                    return a.rearrange("p j e f -> p j (e f)")

                link(nc.vector.scalar_tensor_tensor(flat(tied[:]), flat(diff[:]), 0.0,
                                                    before[:].rearrange("p e f -> p (e f)").unsqueeze(1).broadcast_to([P, TJ, E * E]),
                                                    ALU.is_ge, ALU.mult), g)
                link(nc.vector.scalar_tensor_tensor(flat(outscored[:]), flat(diff[:]), 0.0, flat(tied[:]), ALU.is_gt, ALU.max), g)

            def route(g):
                link(nc.vector.tensor_reduce(rank[:], outscored[:], AX.X, ALU.add), g)
                link(nc.vector.scalar_tensor_tensor(picked[:], rank[:], 1.5, score[:], ALU.is_lt, ALU.mult), g)
                link(nc.vector.tensor_reduce(picked_sum[:], picked[:], AX.X, ALU.add), g)
                link(nc.vector.tensor_scalar(picked_eps[:], picked_sum[:], TOPK_EPS, None, ALU.add), g)
                link(nc.vector.reciprocal(picked_inv[:], picked_eps[:]), g)
                nc.vector.tensor_scalar(combine_scale[:], picked_inv[:], ROUTED_SCALE, None, ALU.mult).then_inc(routed, 1)

            def attend(g):
                dve.wait_ge(pi_ready, after(g))
                for b in range(BPG):
                    ins = nc.vector.tensor_tensor_reduce(out=batch(weighted[:], b), in0=batch(w_sq[:], b), in1=batch(pi_bc[:], b),
                                                         scale=1.0, scalar=0.0, op0=ALU.mult, op1=ALU.add,
                                                         accum_out=dots[:, b:b + 1])
                link(ins, g)
                link(nc.vector.scalar_tensor_tensor(attn_den[:], pi_sum[:], PI_EPS, dots[:], ALU.add, ALU.add), g)
                link(nc.vector.reciprocal(attn_inv[:], attn_den[:]), g)
                link(nc.vector.scalar_tensor_tensor(attn[:], pi_sum[:], PI_EPS, attn_inv[:], ALU.add, ALU.mult), g)
                if not early(g, 2):
                    dve.wait_ge(down_done, count(shift(g, -2), NT, NT))
                for b in range(BPG):
                    ins = nc.vector.scalar_tensor_tensor(batch(attn_out[:, g[1] % 2], b), batch(ps_w[:], b), attn[:, b:b + 1],
                                                         batch(pi_bc[:], b), ALU.mult, ALU.mult)
                ins.then_inc(attn_ready, 1)
                assert step[0] == dve_per_group, step[0]

            def finish(g):
                dve.wait_ge(yT_ready, after(g))
                dve.wait_ge(x_res_loaded[g[1] % 2], loads(g))
                if not early(g, 2):
                    dve.wait_ge(stored[g[1] % 2], loads(shift(g, -2)))
                nc.vector.tensor_tensor(result[:, g[1] % 2], ps_x[:], x_res[:, g[1] % 2], ALU.add).then_inc(result_ready, 1)

            def rest_hidden(g, t):
                m = rows(t)
                dve.wait_ge(hid_hi_ready, count(g, NT, t + 1))
                if not (early(g, 1) and t < SPLIT_RING):
                    dve.wait_ge(down_done, count(g, NT, t + 1 - SPLIT_RING))
                r = t % SPLIT_RING
                nc.vector.tensor_tensor(hid_lo[0:m, r], hidden[0:m, (g[1] * NT + t) % RING], hid_hi[0:m, r], ALU.subtract).then_inc(hid_lo_ready, 1)

            nc.vector.memset(down_raw[MLAST:P, WID - P:], 0.0)
            statistics((0, 0))
            statistics_written((0, 0))
            mean_variance()
            normalise((0, 0))
            rest_x((0, 0))
            dve.wait_ge(setup_transposed, 1)
            dve.wait_ge(small_loaded, 16 * 5)
            dve.wait_ge(consts_done, 1)
            nc.vector.tensor_copy(qkvT[:], ps_w[:, 0:P])
            nc.vector.tensor_copy(routerT[:], ps_w[:, 2 * P:2 * P + E])
            setup_link(nc.vector.tensor_tensor(head_sel[:], head_sel[:], temp_bc[:], ALU.mult))
            nc.vector.tensor_reduce(maxima[:, 3:4], qkvT[:], AX.X, ALU.max, apply_absolute_value=True)
            nc.vector.tensor_reduce(maxima[:, 4:5], routerT[:], AX.X, ALU.max, apply_absolute_value=True)
            dve.wait_ge(gate_loaded, 32)
            nc.vector.tensor_reduce(maxima[:, 0:1], gate_raw[:], AX.X, ALU.max, apply_absolute_value=True)
            dve.wait_ge(up_loaded, 32)
            nc.vector.tensor_reduce(maxima[:, 1:2], up_raw[:], AX.X, ALU.max, apply_absolute_value=True)
            dve.wait_ge(down_loaded, 48)
            nc.vector.tensor_reduce(maxima[:, 2:3], down_raw[:], AX.X, ALU.max, apply_absolute_value=True).then_inc(maxima_ready, 1)
            dve.wait_ge(maxima_spread, 1)
            setup_link(nc.vector.tensor_scalar(clamped[:], max_all[:], 2.0 ** -30, None, ALU.max))
            setup_link(nc.vector.tensor_scalar(power[:].bitcast(U32), clamped[:].bitcast(U32), EXP_MASK, None, ALU.bitwise_and))
            nc.vector.tensor_scalar(alpha[:].bitcast(U32), power[:].bitcast(U32), -1.0, over(14), ALU.mult, ALU.add)
            nc.vector.tensor_scalar(inv_alpha[:], power[:], 2.0 ** -14, None, ALU.mult)
            setup_link(nc.vector.tensor_scalar(gate_pow[:], power[:, 0:1], 2.0 ** -8, None, ALU.max))
            setup_link(nc.vector.tensor_scalar(beta[:].bitcast(U32), gate_pow[:].bitcast(U32), -1.0, over(-17), ALU.mult, ALU.add))
            setup_link(nc.vector.tensor_scalar(gamma[:], beta[:], alpha[:, 1:2], alpha[:, 2:3], ALU.mult, ALU.mult))
            setup_link(nc.vector.tensor_scalar(neg_gamma_q[:], gamma[:], inv_alpha[:, 3:4], -1.0, ALU.mult, ALU.mult))
            setup_link(nc.vector.tensor_scalar(gate_pow[:], gate_pow[:], inv_alpha[:, 1:2], inv_alpha[:, 2:3], ALU.mult, ALU.mult))
            setup_link(nc.vector.tensor_scalar(inv_gamma[:], gate_pow[:], 2.0 ** 17, None, ALU.mult))
            nc.vector.tensor_scalar(woutT[:], ps_w[:, P:2 * P], neg_gamma_q[:, 0:1], None, ALU.mult)
            nc.vector.tensor_scalar(qkv_hi[:], qkvT[:], alpha[:, 3:4], None, ALU.mult)
            setup_link(nc.vector.tensor_scalar(router_hi[:], routerT[:], alpha[:, 4:5], None, ALU.mult))
            nc.vector.scalar_tensor_tensor(qkv_lo[:], qkvT[:], alpha[:, 3:4], qkv_hi[:], ALU.mult, ALU.subtract)
            nc.vector.scalar_tensor_tensor(router_lo[:], routerT[:], alpha[:, 4:5], router_hi[:], ALU.mult,
                                           ALU.subtract).then_inc(scales_ready, 1)
            cols = E * F
            for i, (raw, hi, lo) in enumerate(((gate_raw, gate_hi, gate_lo), (up_raw, up_hi, up_lo))):
                dve.wait_ge(weights_hi, i + 1)
                nc.vector.scalar_tensor_tensor(lo[:, 0:cols].rearrange("d (k p) -> d k p", k=KE),
                                               raw[:, 0:cols].rearrange("d (p k) -> d k p", k=KE), alpha[:, i:i + 1],
                                               hi[:, 0:cols].rearrange("d (k p) -> d k p", k=KE), ALU.mult, ALU.subtract)
                nc.vector.scalar_tensor_tensor(lo[:, cols:cols + FS], raw[:, cols:], alpha[:, i:i + 1],
                                               hi[:, cols:cols + FS], ALU.mult, ALU.subtract).then_inc(weights_ready, 1)
            dve.wait_ge(weights_hi, 3)
            nc.vector.scalar_tensor_tensor(down_lo[:], down_raw[:], alpha[:, 2:3], down_hi[:], ALU.mult,
                                           ALU.subtract).then_inc(weights_ready, 1)
            head_scales((0, 0))
            shift_logits((0, 0))
            rank_experts((0, 0))
            route((0, 0))
            attend((0, 0))
            statistics((0, 1))
            statistics_written((0, 1))
            mean_variance()
            normalise((0, 1))

            def body(g):
                for t in range(NT):
                    n = g[1] * NT + t
                    m = rows(t)
                    if t == 6 and not early(g, 1):
                        finish(shift(g, -1))
                    if ahead_of(g, 1):
                        if t == 0:
                            rest_x(shift(g, 1))
                        if t == 3:
                            head_scales(shift(g, 1))
                        if t == 5:
                            shift_logits(shift(g, 1))
                        if t == 7:
                            rank_experts(shift(g, 1))
                        if t == 8:
                            route(shift(g, 1))
                        if t == 12:
                            attend(shift(g, 1))
                    if ahead_of(g, 2):
                        if t == 4:
                            statistics(shift(g, 2))
                        if t == 5:
                            statistics_written(shift(g, 2))
                        if t == 10:
                            normalise(shift(g, 2))
                    dve.wait_ge(silu_ready, count(g, NT, t + 1))
                    dve.wait_ge(up_ready, count(g, NT, t + 1))
                    if not (early(g, 1) and t < RING):
                        last = back(g, t, RING)
                        dve.wait_ge(hid_hi_ready, count(last[0], NT, last[1] + 1))
                        if last[1] in POOL_REST:
                            rest_taken(dve, *last)
                    nc.vector.scalar_tensor_tensor(hidden[0:m, n % RING], act_gate[0:m, n % RING], beta[0:m, 0:1],
                                                   ps_up[0:m, n % 2], ALU.mult, ALU.mult).then_inc(hid_ready, 1)
                    last = back(g, t, 1)
                    if last[1] not in POOL_REST and not (early(g, 1) and t == 0):
                        rest_hidden(*last)
                    if t == 5 and ahead_of(g, 2):
                        mean_variance()

            run(dve, body)
            finish((0, G - 1))

        @block.tensor
        def _(pe):
            def three(out_ap, hi, lo, m_hi, m_lo, start, stop):
                nc.tensor.matmul(out_ap, hi, m_hi, start=start, stop=False)
                nc.tensor.matmul(out_ap, hi, m_lo, start=False, stop=False)
                return nc.tensor.matmul(out_ap, lo, m_hi, start=False, stop=stop)

            def transpose_x(g):
                pe.wait_ge(xn_ready, after(g))
                if not early(g, 1):
                    pe.wait_ge(pi_ready, after(g, 0))
                for j in range(TJ):
                    ins = nc.tensor.transpose(ps_x[:, j * P:(j + 1) * P], xn[:, j], ident[:])
                ins.then_inc(xT_ready, 1)

            def project_w(g):
                q = g[1] % 2
                pe.wait_ge(lo_x_ready, after(g))
                if not early(g, 1):
                    pe.wait_ge(combine_ready, after(g, 0))
                    pe.wait_ge(attn_ready, after(g, 0))
                at = TJ * BPG * H
                for j in range(TJ):
                    c = slice(j * P, (j + 1) * P)
                    o = ps_s[:, at + j * E:at + (j + 1) * E]
                    nc.tensor.matmul(o, xT_hi[:, q, c], router_hi[:], start=True, stop=False)
                    nc.tensor.matmul(o, xT_hi[:, q, c], router_lo[:], start=False, stop=False)
                    nc.tensor.matmul(o, xT_lo[:, q, c], router_hi[:], start=False, stop=True)
                three(ps_w[:], qkv_hi[:], qkv_lo[:], xT_hi[:, q], xT_lo[:, q], True, True).then_inc(w_ready, 1)

            def head_logits(g):
                pe.wait_ge(head_scaled_ready, after(g))
                for j in range(TJ):
                    w = BPG * H
                    ins = nc.tensor.matmul(ps_s[:, j * w:(j + 1) * w], w_sq[:, j * P:(j + 1) * P],
                                           head_scaled[:].rearrange("p b h -> p (b h)"), start=True, stop=True)
                ins.then_inc(logits_ready, 1)

            def spread(g):
                pe.wait_ge(wide_ready, after(g))
                if not early(g, 2):
                    pe.wait_ge(result_ready, after(g, -1))
                for j in range(TJ):
                    c = slice(j * P, (j + 1) * P)
                    nc.tensor.transpose(ps_x[:, c], pi_wide[:, j].rearrange("p h d -> p (h d)"), ident[:])
                    ins = nc.tensor.transpose(ps_s[:, c], combine_wide[:, j].rearrange("p e f -> p (e f)"), ident[:])
                ins.then_inc(spread_ready, 1)

            def down(g, t):
                m = rows(t)
                r = t % SPLIT_RING
                c = slice(t * P, (t + 1) * P)
                rest_taken(pe, g, t)
                if t == 0 and not early(g, 1):
                    pe.wait_ge(y_taken, after(g, 0))
                if t == NT - 2:
                    pe.wait_ge(attn_ready, after(g))
                    nc.tensor.matmul(ps_y[:], woutT[:], attn_out[:, g[1] % 2], start=False, stop=False)
                three(ps_y[:], down_hi[0:m, c], down_lo[0:m, c], hid_hi[0:m, r], hid_lo[0:m, r],
                      t == 0, t == NT - 1).then_inc(down_done, 1)

            def transpose_y(g):
                pe.wait_ge(y_taken, after(g))
                if ahead_of(g, 1):
                    pe.wait_ge(lo_x_ready, after(shift(g, 1)))
                for j in range(TJ):
                    ins = nc.tensor.transpose(ps_x[:, j * P:(j + 1) * P], yT[:, j * P:(j + 1) * P], ident[:])
                ins.then_inc(yT_ready, 1)

            pe.wait_ge(consts_done, 1)
            transpose_x((0, 0))
            pe.wait_ge(small_loaded, 16 * 5)
            nc.tensor.transpose(ps_w[:, 0:P], qkv_raw[:], ident[:])
            nc.tensor.transpose(ps_w[:, P:2 * P], out_raw[:], ident[:])
            nc.tensor.transpose(ps_w[:, 2 * P:2 * P + E], router_raw[:], ident[0:E, 0:E]).then_inc(setup_transposed, 1)
            pe.wait_ge(scales_ready, 1)
            project_w((0, 0))
            head_logits((0, 0))
            spread((0, 0))
            pe.wait_ge(weights_ready, 3)

            def gate(g, t):
                c, m, n = slice(t * P, t * P + rows(t)), rows(t), g[1] * NT + t
                if not (early(g, 1) and t < 2):
                    pe.wait_ge(silu_ready, count(g, NT, t - 1))
                three(ps_gate[0:m, n % 2], gate_hi[:, c], gate_lo[:, c], xT_hi[:, g[1] % 2], xT_lo[:, g[1] % 2],
                      True, True).then_inc(gate_ready, 1)

            def up(g, t):
                c, m, n = slice(t * P, t * P + rows(t)), rows(t), g[1] * NT + t
                if not (early(g, 1) and t < 2):
                    pe.wait_ge(hid_ready, count(g, NT, t - 1))
                three(ps_up[0:m, n % 2], up_hi[:, c], up_lo[:, c], xT_hi[:, g[1] % 2], xT_lo[:, g[1] % 2],
                      True, True).then_inc(up_ready, 1)

            def body(g):
                for t in range(NT):
                    gate(g, t)
                    if t >= 1:
                        up(g, t - 1)
                    elif not early(g, 1):
                        up(shift(g, -1), NT - 1)
                    if t >= LAG:
                        down(g, t - LAG)
                    elif not early(g, 1):
                        down(shift(g, -1), t + NT - LAG)
                    if ahead_of(g, 1):
                        if t == 0:
                            transpose_x(shift(g, 1))
                        if t == 2:
                            project_w(shift(g, 1))
                        if t == 4:
                            head_logits(shift(g, 1))
                        if t == 11:
                            spread(shift(g, 1))
                    if t == LAG and not early(g, 1):
                        transpose_y(shift(g, -1))

            run(pe, body)
            up((0, G - 1), NT - 1)
            for t in range(NT - LAG, NT):
                down((0, G - 1), t)
            transpose_y((0, G - 1))


_INS = ['L0_attn_x', 'L0_attn_Wqkv', 'L0_attn_temp', 'L0_attn_Wout', 'L0_attn_bout', 'L0_ffn_gate_w', 'L0_ffn_w_gate',
        'L0_ffn_w_up', 'L0_ffn_w_down', 'L0_ffn_sw_gate', 'L0_ffn_sw_up', 'L0_ffn_sw_down']


def kernel(**inputs):
    import numpy as np
    import concourse.bacc as bacc
    from concourse.bass_utils import run_bass_kernel_spmd

    nc = bacc.Bacc("TRN2", target_bir_lowering=False, num_devices=1)
    arrays, args = {}, []
    for name in _INS:
        a = np.ascontiguousarray(inputs[name])
        arrays[f"in_{name}"] = a
        args.append(nc.dram_tensor(f"in_{name}", a.shape, mybir.dt.from_np(a.dtype), kind="ExternalInput").ap())
    out = nc.dram_tensor("out", arrays["in_L0_attn_x"].shape, F32, kind="ExternalOutput").ap()
    attn_moe_kernel(nc, *args, out)
    r = run_bass_kernel_spmd(nc, [arrays], core_ids=[0])
    return r.results[0]["out"]
```

```python
from contextlib import ExitStack

import concourse.bass as bass
from concourse import mybir

ALU = mybir.AluOpType
ACT = mybir.ActivationFunctionType
AX = mybir.AxisListType
F32 = mybir.dt.float32
F16 = mybir.dt.float16
U32 = mybir.dt.uint32

P = 128
BLK = 512
TJ = BLK // P
LN_EPS = 1e-5
NORM_EPS_SQ = 1e-12 ** 2
PI_EPS = 1e-8
TOPK_EPS = 1e-20
ROUTED_SCALE = 2.5
LAG = 8
RING = 7
GATE_RING = 4
HI_LAG = 2
LO_LAG = 2
SPLIT_RING = 7
POOL_REST = (0, 1, 2, 5)

STEADY = dict(transpose_x=0, split_x=0, rest_x=0, project_w=2, square_w=3, head_scales=3, head_logits=4, shift_logits=5,
              exponentials=6, rank_experts=7, statistics=3, layer_norm=6, normalise=10, route=8, widen=8, spread=12, take_spread=13, attend=13)
NEXT = dict(transpose_x=1, split_x=1, rest_x=1, project_w=5, square_w=6, head_scales=5, head_logits=7, shift_logits=7,
            exponentials=8, rank_experts=8, statistics=4, layer_norm=6, normalise=12, route=9, widen=9, spread=13, take_spread=13, attend=13)
OWN = dict(head_logits=0, rank_experts=0, route=0, spread=3, take_spread=4, attend=3,
           largest_down=1, spread_maxima=2, down_scales=3, down_hi=5, down_lo=5)

EXP_MASK = 0x7F800000


def over(k):
    return float((254 + k) << 23)


def attn_moe_kernel(nc, x, Wqkv, temp, Wout, bout, gate_w, w_gate, w_up, w_down, sw_gate, sw_up, sw_down, out):
    NB, N, D = x.shape
    E, _, F = w_gate.shape
    FS = sw_gate.shape[1]
    H = temp.shape[0]
    HD = D // H
    G = NB * N // BLK
    BPG = BLK // N
    ROWS = N // TJ
    KE = F * E // P
    ER = P // E
    SH = -(-FS // P)
    NT = SH + KE
    PART = FS - (SH - 1) * P
    assert D == P and F == ER * KE and BPG * ROWS == P and G % 2 == 0 and G >= 6 and NT % 2 == 0 and NT % SPLIT_RING == 0 and NT % RING == 0 and 2 * NT % GATE_RING == 0 and BPG == 2
    WID = NT * P
    QKV, ROUTER, GATE, UP, DOWN = range(5)

    x_view = x.rearrange("b n d -> (b n) d").rearrange("(g p j) d -> g p (j d)", p=P, j=TJ)
    out_view = out.rearrange("b n d -> (b n) d").rearrange("(g p j) d -> g p (j d)", p=P, j=TJ)

    with ExitStack() as ctx:
        def sb(name, shape, dt=F32):
            return ctx.enter_context(nc.sbuf_tensor(name, shape, dt))

        def ps(name, shape, dt=F32):
            return ctx.enter_context(nc.psum_tensor(name, shape, dt))

        def sem(name):
            return ctx.enter_context(nc.semaphore(name))

        gate_raw = sb("gate_raw", [P, FS + E * F])
        up_raw = sb("up_raw", [P, FS + E * F])
        down_raw = sb("down_raw", [P, WID])
        up_scaled_raw = sb("up_scaled_raw", [P, WID])
        qkv_raw = sb("qkv_raw", [P, P])
        out_raw = sb("out_raw", [P, P])
        router_raw = sb("router_raw", [E, P])
        gate_hi = sb("gate_hi", [P, WID], F16)
        gate_lo = sb("gate_lo", [P, WID], F16)
        up_hi = sb("up_hi", [P, WID], F16)
        up_lo = sb("up_lo", [P, WID], F16)
        down_hi = sb("down_hi", [P, WID], F16)
        down_lo = sb("down_lo", [P, WID], F16)
        qkv_hi = sb("qkv_hi", [P, P], F16)
        qkv_lo = sb("qkv_lo", [P, P], F16)
        router_hi = sb("router_hi", [P, E], F16)
        router_lo = sb("router_lo", [P, E], F16)
        qkvT = sb("qkvT", [P, P])
        routerT = sb("routerT", [P, E])
        woutT_raw = sb("woutT_raw", [P, P])
        woutT = sb("woutT", [P, P])
        temp_bc = sb("temp_bc", [P, H])
        bias_col = sb("bias_col", [P, 1])

        ident = sb("ident", [P, P])
        head_sel = sb("head_sel", [P, H])
        before = sb("before", [P, E, E])
        neg_half = sb("neg_half", [P, TJ])
        ln_eps = sb("ln_eps", [P, TJ])
        maxima = sb("maxima", [P, 5])               
        max_all = sb("max_all", [P, 5])
        clamped = sb("clamped", [P, 5])
        power = sb("power", [P, 5])
        alpha = sb("alpha", [P, 5])
        inv_alpha = sb("inv_alpha", [P, 5])
        gate_pow = sb("gate_pow", [P, 1])
        beta = sb("beta", [P, 1])
        gamma = sb("gamma", [P, 1])
        inv_gamma = sb("inv_gamma", [P, 1])
        neg_gamma_q = sb("neg_gamma_q", [P, 1])

        x_in = sb("x_in", [P, 2, TJ, P])
        x_res = sb("x_res", [P, 2, BLK])
        stats = sb("stats", [P, TJ, 6])
        mean_var = sb("mean_var", [P, TJ, 2])
        var_eps = sb("var_eps", [P, TJ])
        rstd = sb("rstd", [P, TJ])
        xn = sb("xn", [P, TJ, P])
        xT_hi = sb("xT_hi", [P, 2, BLK], F16)
        xT_lo = sb("xT_lo", [P, 2, BLK], F16)
        w_sq = sb("w_sq", [P, BLK])
        norm_sq = sb("norm_sq", [P, BPG])
        norm_max = sb("norm_max", [P, BPG])
        norm_inv = sb("norm_inv", [P, BPG])
        head_scaled = sb("head_scaled", [P, BPG, H])
        logits = sb("logits", [P, TJ, H + E])
        top = sb("top", [P, TJ, 2])
        shifted = sb("shifted", [P, TJ, H + E])
        expd = sb("expd", [P, TJ, H + E])
        sums = sb("sums", [P, TJ, 2])
        sums_inv = sb("sums_inv", [P, TJ, 2])
        score = sb("score", [P, TJ, E])
        diff = sb("diff", [P, TJ, E, E])
        tied = sb("tied", [P, TJ, E, E])
        outscored = sb("outscored", [P, TJ, E, E])
        rank = sb("rank", [P, TJ, E])
        picked = sb("picked", [P, TJ, E])
        picked_sum = sb("picked_sum", [P, TJ])
        picked_eps = sb("picked_eps", [P, TJ])
        picked_inv = sb("picked_inv", [P, TJ])
        combine_scale = sb("combine_scale", [P, TJ])
        pi_wide = sb("pi_wide", [P, TJ, H, HD])
        combine_wide = sb("combine_wide", [P, TJ, E, ER])
        pi_bc = sb("pi_bc", [P, BLK])
        pi_sum = sb("pi_sum", [P, BPG])
        weighted = sb("weighted", [P, BLK])
        dots = sb("dots", [P, BPG])
        attn_den = sb("attn_den", [P, BPG])
        attn_inv = sb("attn_inv", [P, BPG])
        attn = sb("attn", [P, BPG])
        attn_out = sb("attn_out", [P, 2, BLK])
        combine_bc = sb("combine_bc", [P, 2, BLK])

        act_gate = sb("act_gate", [P, GATE_RING, BLK])
        hidden = sb("hidden", [P, RING, BLK])
        hid_hi = sb("hid_hi", [P, SPLIT_RING, BLK], F16)
        hid_lo = sb("hid_lo", [P, SPLIT_RING, BLK], F16)
        yT = sb("yT", [P, BLK])
        result = sb("result", [P, 2, BLK])

        ps_gate = ps("ps_gate", [P, 2, BLK])
        ps_up = ps("ps_up", [P, 2, BLK])
        ps_y = ps("ps_y", [P, BLK])
        ps_x = ps("ps_x", [P, BLK])
        ps_w = ps("ps_w", [P, BLK])
        ps_s = ps("ps_s", [P, BLK])

        x_in_loaded = [sem("x_in_loaded0"), sem("x_in_loaded1")]
        x_res_loaded = [sem("x_res_loaded0"), sem("x_res_loaded1")]
        stored = [sem("stored0"), sem("stored1")]
        projections_loaded, small_loaded = sem("projections_loaded"), sem("small_loaded")
        gate_loaded, up_loaded, down_loaded = sem("gate_loaded"), sem("up_loaded"), sem("down_loaded")
        consts_step, consts_done = sem("consts_step"), sem("consts_done")
        setup_transposed = sem("setup_transposed")
        setup_step = sem("setup_step")
        maxima_ready, maxima_spread = sem("maxima_ready"), sem("maxima_spread")
        transposes_taken, projections_ready = sem("transposes_taken"), sem("projections_ready")
        scales_ready, down_scales_ready = sem("scales_ready"), sem("down_scales_ready")
        up_scaled = sem("up_scaled")
        weights_hi, weights_ready, pool_weights_ready = sem("weights_hi"), sem("weights_ready"), sem("pool_weights_ready")
        stats_written = sem("stats_written")
        dve_step = sem("dve_step")
        pool_step = sem("pool_step")
        stats_ready, rstd_ready, xn_ready = sem("stats_ready"), sem("rstd_ready"), sem("xn_ready")
        xT_ready, hi_x_ready, lo_x_ready = sem("xT_ready"), sem("hi_x_ready"), sem("lo_x_ready")
        w_ready, wsq_ready, head_scaled_ready = sem("w_ready"), sem("wsq_ready"), sem("head_scaled_ready")
        logits_ready, shifted_ready, exp_ready = sem("logits_ready"), sem("shifted_ready"), sem("exp_ready")
        routed, wide_ready, spread_ready = sem("routed"), sem("wide_ready"), sem("spread_ready")
        pi_ready, combine_ready, attn_ready = sem("pi_ready"), sem("combine_ready"), sem("attn_ready")
        gate_ready, up_ready, silu_ready = sem("gate_ready"), sem("up_ready"), sem("silu_ready")
        combined, hid_ready = sem("combined"), sem("hid_ready")
        hid_hi_ready, down_done = sem("hid_hi_ready"), sem("down_done")
        hid_lo_ready, pool_lo_ready = sem("hid_lo_ready"), sem("pool_lo_ready")
        y_taken, yT_ready, result_ready = sem("y_taken"), sem("yT_ready"), sem("result_ready")

        def count(g, per, k):
            m, c = g
            return m * (2 * per) + (c * per + k)

        def after(g, k=1):
            return count(g, 1, k)

        def loads(g):
            m, c = g
            return m * 16 + 16 * (c // 2 + 1)

        def shift(g, by):
            return (g[0], g[1] + by)

        def fixed(g):
            return isinstance(g[0], int)

        def early(g, n):
            return fixed(g) and 2 * g[0] + g[1] < n

        def batch(ap, b):
            return ap.rearrange("p (j b q) -> p b j q", j=TJ, b=BPG)[:, b]

        def weighed(eng, g, t):
            if t >= SH:
                eng.wait_ge(combined, count(g, KE, t + 1 - SH))
            else:
                eng.wait_ge(hid_ready, count(g, NT, t + 1))

        def rest_taken(eng, g, t, by=None):
            if t in POOL_REST:
                eng.wait_ge(pool_lo_ready, count(g, len(POOL_REST), 1 + POOL_REST.index(t)))
            else:
                eng.wait_ge(hid_lo_ready, count(g, NT - len(POOL_REST), 1 + sum(u not in POOL_REST for u in range(t))))

        def back(g, t, by):
            return (g, t - by) if t >= by else (shift(g, -1), t - by + NT)

        def routed_columns(raw):
            return raw[:, FS:].rearrange("d (p k) -> d k p", k=KE)

        def routed_tiles(half):
            return half[:, SH * P:].rearrange("d (k p) -> d k p", k=KE)

        def rows(t):
            return PART if t == SH - 1 else P

        def rows_of(g):
            return x_view[g[0] * 2 + g[1]], out_view[g[0] * 2 + g[1]]

        def run(eng, body):
            body((0, 0))
            with eng.Fori(0, (G - 4) // 2) as m:
                body((m, 1))
                body((m, 2))
            for c in range(G - 3, G):
                body((0, c))

        def slot(g, step):
            return (NEXT if early(g, 1) else STEADY)[step]

        def own(g, step):
            return OWN[step] if early(g, 1) else None

        def ahead_of(g, by):
            return not fixed(g) or g[1] + by < G

        block = ctx.enter_context(nc.Block())

        @block.sync
        def _(sp):
            def load_x_in(g):
                if not early(g, 2):
                    sp.wait_ge(xn_ready, after(shift(g, -2)))
                sp.dma_start(x_in[:, g[1] % 2].rearrange("p j d -> p (j d)"), rows_of(g)[0]).then_inc(x_in_loaded[g[1] % 2], 16)

            def load_x_res(g):
                if not early(g, 2):
                    sp.wait_ge(result_ready, after(shift(g, -2)))
                sp.dma_start(x_res[:, g[1] % 2], rows_of(g)[0]).then_inc(x_res_loaded[g[1] % 2], 16)

            def store(g):
                sp.wait_ge(result_ready, after(g))
                sp.dma_start(rows_of(g)[1], result[:, g[1] % 2]).then_inc(stored[g[1] % 2], 16)

            full = FS - PART
            load_x_in((0, 0))
            sp.dma_start(gate_raw[:, 0:FS], sw_gate).then_inc(gate_loaded, 16)
            sp.dma_start(gate_raw[:, FS:].rearrange("d (e f) -> d e f", e=E),
                         w_gate.rearrange("e d f -> d e f")).then_inc(gate_loaded, 16)
            sp.dma_start(router_raw[:], gate_w).then_inc(projections_loaded, 16)
            sp.dma_start(qkv_raw[:], Wqkv).then_inc(projections_loaded, 16)
            sp.dma_start(out_raw[:], Wout).then_inc(projections_loaded, 16)
            sp.dma_start(up_raw[:, 0:FS], sw_up).then_inc(up_loaded, 16)
            sp.dma_start(up_raw[:, FS:].rearrange("d (e f) -> d e f", e=E),
                         w_up.rearrange("e d f -> d e f")).then_inc(up_loaded, 16)
            load_x_in((0, 1))
            sp.dma_start(down_raw[:, 0:full].rearrange("p (k d) -> p k d", d=P),
                         sw_down[0:full, :].rearrange("(k p) d -> p k d", p=P)).then_inc(down_loaded, 16)
            sp.dma_start(down_raw[0:PART, full:SH * P], sw_down[full:, :]).then_inc(down_loaded, 16)
            sp.dma_start(down_raw[:, SH * P:],
                         w_down.rearrange("e f d -> (e f) d").rearrange("(p k) d -> p (k d)", k=KE)).then_inc(down_loaded, 16)
            load_x_in((0, 2))
            load_x_res((0, 0))

            def body(g):
                if ahead_of(g, 3):
                    load_x_in(shift(g, 3))
                if ahead_of(g, 1):
                    load_x_res(shift(g, 1))
                if not early(g, 1):
                    store(shift(g, -1))

            run(sp, body)
            store((0, G - 1))
            for half in stored:
                sp.wait_ge(half, 16 * (G // 2))

        @block.gpsimd
        def _(pool):
            nc.gpsimd.memset(ident[:], 0.0).then_inc(consts_step, 1)
            nc.gpsimd.memset(head_sel[:], 1.0).then_inc(consts_step, 1)
            nc.gpsimd.memset(before[:], 1.0).then_inc(consts_step, 1)
            nc.gpsimd.memset(neg_half[:], -0.5).then_inc(consts_step, 1)
            nc.gpsimd.memset(ln_eps[:], LN_EPS).then_inc(consts_step, 1)
            pool.wait_ge(consts_step, 3)
            nc.gpsimd.affine_select(out=ident[:], in_=ident[:], compare_op=ALU.not_equal, fill=1.0, base=0,
                                    pattern=[[-1, P]], channel_multiplier=1).then_inc(consts_step, 1)
            nc.gpsimd.affine_select(out=before[:], in_=before[:], compare_op=ALU.is_gt, fill=0.0, base=0,
                                    pattern=[[1, E], [-1, E]], channel_multiplier=0).then_inc(consts_step, 1)
            nc.gpsimd.affine_select(out=head_sel[:], in_=head_sel[:], compare_op=ALU.is_ge, fill=0.0, base=0,
                                    pattern=[[-HD, H]], channel_multiplier=1).then_inc(consts_step, 1)
            pool.wait_ge(consts_step, 8)
            nc.gpsimd.affine_select(out=head_sel[:], in_=head_sel[:], compare_op=ALU.is_gt, fill=0.0, base=HD,
                                    pattern=[[HD, H]], channel_multiplier=-1).then_inc(consts_done, 1)

            def layer_norm(g):
                pool.wait_ge(stats_ready, after(g))
                nc.gpsimd.tensor_tensor(var_eps[:], mean_var[:, :, 1], ln_eps[:], ALU.add).then_inc(pool_step, 1)
                pool.wait_ge(pool_step, after(g))
                nc.gpsimd.tensor_tensor(rstd[:], var_eps[:], neg_half[:], ALU.pow).then_inc(rstd_ready, 1)

            def widen(g):
                pool.wait_ge(routed, after(g))
                nc.gpsimd.tensor_tensor(pi_wide[:], expd[:, :, 0:H].unsqueeze(3).broadcast_to([P, TJ, H, HD]),
                                        sums_inv[:, :, 0:1].unsqueeze(3).broadcast_to([P, TJ, H, HD]), ALU.mult)
                nc.gpsimd.tensor_tensor(combine_wide[:], picked[:].unsqueeze(3).broadcast_to([P, TJ, E, ER]),
                                        combine_scale[:].unsqueeze(2).unsqueeze(3).broadcast_to([P, TJ, E, ER]), ALU.mult).then_inc(wide_ready, 1)

            layer_norm((0, 0))
            def spread_maxima(i):
                pool.wait_ge(maxima_ready, i + 1)
                c = (slice(QKV, DOWN), slice(DOWN, 5))[i]
                nc.gpsimd.partition_all_reduce(max_all[:, c], maxima[:, c], P,
                                               bass.bass_isa.ReduceOp.max).then_inc(maxima_spread, 1)

            spread_maxima(0)
            pool.wait_ge(scales_ready, 1)
            nc.gpsimd.tensor_tensor(routed_tiles(up_scaled_raw), routed_columns(up_raw),
                                    alpha[:, UP:UP + 1].unsqueeze(2).broadcast_to([P, KE, P]), ALU.mult).then_inc(up_scaled, 1)
            layer_norm((0, 1))
            pool.wait_ge(up_scaled, 1)
            pool.wait_ge(weights_hi, 4)
            nc.gpsimd.tensor_tensor(routed_tiles(up_lo), routed_tiles(up_scaled_raw), routed_tiles(up_hi),
                                    ALU.subtract).then_inc(pool_weights_ready, 1)
            widen((0, 0))

            def rest_hidden(g, t):
                m, r = rows(t), t % SPLIT_RING
                pool.wait_ge(hid_hi_ready, count(g, NT, t + 1))
                if not (early(g, 1) and t < SPLIT_RING):
                    pool.wait_ge(down_done, count(g, NT, t + 1 - SPLIT_RING))
                nc.gpsimd.tensor_tensor(hid_lo[0:m, r], hidden[0:m, t % RING], hid_hi[0:m, r],
                                        ALU.subtract).then_inc(pool_lo_ready, 1)

            def body(g):
                for t in range(NT):
                    if t >= SH:
                        pool.wait_ge(hid_ready, count(g, NT, t + 1))
                        if t == SH:
                            pool.wait_ge(combine_ready, after(g))
                        h = hidden[:, t % RING]
                        nc.gpsimd.tensor_tensor(h, h, combine_bc[:, g[1] % 2], ALU.mult).then_inc(combined, 1)
                    before_g, before_t = back(g, t, LO_LAG)
                    if before_t in POOL_REST and not (early(g, 1) and t < LO_LAG):
                        rest_hidden(before_g, before_t)
                    if t == own(g, 'spread_maxima'):
                        spread_maxima(1)
                    if t == slot(g, 'layer_norm') and ahead_of(g, 2):
                        layer_norm(shift(g, 2))
                    if t == slot(g, 'widen') and ahead_of(g, 1):
                        widen(shift(g, 1))

            run(pool, body)

        @block.scalar
        def _(act):
            act.dma_start(temp_bc[:], temp.rearrange("h o -> o h").broadcast_to([P, H])).then_inc(small_loaded, 16)
            act.dma_start(bias_col[:], bout.rearrange("(d o) -> d o", o=1)).then_inc(small_loaded, 16)

            def split_x(g):
                act.wait_ge(xT_ready, after(g))
                nc.scalar.activation(xT_hi[:, g[1] % 2], ps_x[:], ACT.Copy).then_inc(hi_x_ready, 1)

            def square_w(g):
                act.wait_ge(w_ready, after(g))
                for b in range(BPG):
                    ins = nc.scalar.activation(batch(w_sq[:], b), batch(ps_w[:], b), ACT.Square,
                                               scale=inv_alpha[:, QKV:QKV + 1], accum_out=norm_sq[:, b:b + 1])
                ins.then_inc(wsq_ready, 1)

            def exponentials(g):
                act.wait_ge(shifted_ready, after(g))
                nc.scalar.activation(expd[:], shifted[:], ACT.Exp).then_inc(exp_ready, 1)

            def take_spread(g):
                act.wait_ge(spread_ready, after(g))
                for b in range(BPG):
                    ins = nc.scalar.activation(batch(pi_bc[:], b), batch(ps_x[:], b), ACT.Copy,
                                               accum_out=pi_sum[:, b:b + 1])
                ins.then_inc(pi_ready, 1)
                nc.scalar.activation(combine_bc[:, g[1] % 2], ps_s[:], ACT.Copy).then_inc(combine_ready, 1)

            def take_y(g):
                act.wait_ge(down_done, count(g, NT, NT))
                if not early(g, 1):
                    act.wait_ge(yT_ready, after(g, 0))
                nc.scalar.activation(yT[:], ps_y[:], ACT.Identity, bias=bias_col[:, 0:1],
                                     scale=inv_gamma[:, 0:1]).then_inc(y_taken, 1)

            def split_hidden(g, t):
                m = rows(t)
                weighed(act, g, t)
                if not (early(g, 1) and t < SPLIT_RING):
                    act.wait_ge(down_done, count(g, NT, t + 1 - SPLIT_RING))
                nc.scalar.activation(hid_hi[0:m, t % SPLIT_RING], hidden[0:m, t % RING], ACT.Copy).then_inc(hid_hi_ready, 1)

            def high_half(dst, raw, k):
                nc.scalar.activation(dst[:, 0:FS], raw[:, 0:FS], ACT.Copy, scale=alpha[:, k:k + 1]).then_inc(weights_hi, 1)

            def high_half_routed(dst, raw, k):
                nc.scalar.activation(routed_tiles(dst), routed_columns(raw), ACT.Copy, scale=alpha[:, k:k + 1]).then_inc(weights_hi, 1)

            act.wait_ge(setup_transposed, 1)
            nc.scalar.activation(qkvT[:], ps_w[:, 0:P], ACT.Copy)
            nc.scalar.activation(woutT_raw[:], ps_w[:, P:2 * P], ACT.Copy)
            nc.scalar.activation(routerT[:], ps_w[:, 2 * P:2 * P + E], ACT.Copy).then_inc(transposes_taken, 1)
            split_x((0, 0))
            act.wait_ge(scales_ready, 1)
            high_half(gate_hi, gate_raw, GATE)
            high_half(up_hi, up_raw, UP)
            high_half_routed(gate_hi, gate_raw, GATE)
            square_w((0, 0))
            high_half_routed(up_hi, up_raw, UP)
            split_x((0, 1))
            exponentials((0, 0))

            def body(g):
                for t in range(NT):
                    if ahead_of(g, 1):
                        if t == slot(g, 'square_w'):
                            square_w(shift(g, 1))
                        if t == slot(g, 'exponentials'):
                            exponentials(shift(g, 1))
                        if t == slot(g, 'take_spread'):
                            take_spread(shift(g, 1))
                    if early(g, 1):
                        if t == OWN['down_hi']:
                            act.wait_ge(down_scales_ready, 1)
                            nc.scalar.activation(down_hi[:], down_raw[:], ACT.Copy, scale=alpha[:, DOWN:DOWN + 1]).then_inc(weights_hi, 1)
                        if t == OWN['take_spread']:
                            take_spread(g)
                    act.wait_ge(gate_ready, count(g, NT, t + 1))
                    if not (early(g, 1) and t < GATE_RING):
                        act.wait_ge(hid_ready, count(g, NT, t + 1 - GATE_RING))
                    n = g[1] * NT + t
                    m = rows(t)
                    nc.scalar.activation(act_gate[0:m, n % GATE_RING], ps_gate[0:m, n % 2], ACT.Silu,
                                         scale=inv_alpha[0:m, GATE:GATE + 1]).then_inc(silu_ready, 1)
                    if t == slot(g, 'split_x') and ahead_of(g, 1) and not early(g, 1):
                        act.wait_ge(up_ready, count(g, NT, 0))
                        split_x(shift(g, 1))
                    if t == LAG - 1 and not early(g, 1):
                        take_y(shift(g, -1))
                    if not (early(g, 1) and t < HI_LAG):
                        split_hidden(*back(g, t, HI_LAG))

            run(act, body)
            for t in range(NT - HI_LAG, NT):
                split_hidden((0, G - 1), t)
            take_y((0, G - 1))

        @block.vector
        def _(dve):
            dve_per_group = 19
            step = [0]

            def link(ins, g):
                step[0] += 1
                ins.then_inc(dve_step, 1)
                dve.wait_ge(dve_step, count(g, dve_per_group, step[0]))

            set_up = [0]

            def setup_link(ins):
                set_up[0] += 1
                ins.then_inc(setup_step, 1)
                dve.wait_ge(setup_step, set_up[0])

            def statistics(g):
                dve.wait_ge(x_in_loaded[g[1] % 2], loads(g))
                for j in range(TJ):
                    ins = nc.vector.bn_stats(stats[:, j], x_in[:, g[1] % 2, j])
                ins.then_inc(stats_written, 1)

            def statistics_written(g):
                dve.wait_ge(stats_written, after(g))

            def mean_variance():
                for j in range(TJ):
                    ins = nc.vector.bn_aggr(mean_var[:, j], stats[:, j])
                ins.then_inc(stats_ready, 1)

            def normalise(g):
                dve.wait_ge(rstd_ready, after(g))
                for j in range(TJ):
                    ins = nc.vector.tensor_scalar(xn[:, j], x_in[:, g[1] % 2, j], mean_var[:, j, 0:1], rstd[:, j:j + 1],
                                                  ALU.subtract, ALU.mult)
                ins.then_inc(xn_ready, 1)

            def rest_x(g):
                dve.wait_ge(hi_x_ready, after(g))
                nc.vector.tensor_tensor(xT_lo[:, g[1] % 2], ps_x[:], xT_hi[:, g[1] % 2], ALU.subtract).then_inc(lo_x_ready, 1)

            def head_scales(g):
                step[0] = 0
                dve.wait_ge(wsq_ready, after(g))
                link(nc.vector.tensor_scalar(norm_max[:], norm_sq[:], NORM_EPS_SQ, None, ALU.max), g)
                link(nc.vector.reciprocal(norm_inv[:], norm_max[:]), g)
                for b in range(BPG):
                    ins = nc.vector.tensor_scalar(head_scaled[:, b], head_sel[:], norm_inv[:, b:b + 1], None, ALU.mult)
                ins.then_inc(head_scaled_ready, 1)

            def shift_logits(g):
                dve.wait_ge(logits_ready, after(g))
                raw = ps_s[:, 0:TJ * BPG * H].rearrange("p (j b h) -> p j b h", j=TJ, b=BPG)
                for b in range(BPG):
                    r = slice(b * ROWS, (b + 1) * ROWS)
                    nc.vector.tensor_copy(logits[r, :, 0:H], raw[r, :, b])
                ins = nc.vector.tensor_scalar(logits[:, :, H:],
                                              ps_s[:, TJ * BPG * H:TJ * (BPG * H + E)].rearrange("p (j e) -> p j e", j=TJ),
                                              inv_alpha[:, ROUTER:ROUTER + 1], None, ALU.mult)
                link(ins, g)
                nc.vector.tensor_reduce(top[:, :, 0], logits[:, :, 0:H], AX.X, ALU.max)
                link(nc.vector.tensor_reduce(top[:, :, 1], logits[:, :, H:], AX.X, ALU.max), g)
                nc.vector.tensor_tensor(shifted[:, :, 0:H], logits[:, :, 0:H], top[:, :, 0:1].broadcast_to([P, TJ, H]), ALU.subtract)
                nc.vector.tensor_tensor(shifted[:, :, H:], logits[:, :, H:], top[:, :, 1:2].broadcast_to([P, TJ, E]),
                                        ALU.subtract).then_inc(shifted_ready, 1)

            def rank_experts(g):
                dve.wait_ge(exp_ready, after(g))
                nc.vector.tensor_reduce(sums[:, :, 0], expd[:, :, 0:H], AX.X, ALU.add)
                link(nc.vector.tensor_reduce(sums[:, :, 1], expd[:, :, H:], AX.X, ALU.add), g)
                link(nc.vector.reciprocal(sums_inv[:], sums[:]), g)
                link(nc.vector.tensor_tensor(score[:], expd[:, :, H:], sums_inv[:, :, 1:2].broadcast_to([P, TJ, E]), ALU.mult), g)
                link(nc.vector.tensor_tensor(diff[:], score[:].unsqueeze(2).broadcast_to([P, TJ, E, E]),
                                             score[:].unsqueeze(3).broadcast_to([P, TJ, E, E]), ALU.subtract), g)

                def flat(a):
                    return a.rearrange("p j e f -> p j (e f)")

                link(nc.vector.scalar_tensor_tensor(flat(tied[:]), flat(diff[:]), 0.0,
                                                    before[:].rearrange("p e f -> p (e f)").unsqueeze(1).broadcast_to([P, TJ, E * E]),
                                                    ALU.is_ge, ALU.mult), g)
                link(nc.vector.scalar_tensor_tensor(flat(outscored[:]), flat(diff[:]), 0.0, flat(tied[:]), ALU.is_gt, ALU.max), g)

            def route(g):
                link(nc.vector.tensor_reduce(rank[:], outscored[:], AX.X, ALU.add), g)
                link(nc.vector.scalar_tensor_tensor(picked[:], rank[:], 1.5, score[:], ALU.is_lt, ALU.mult), g)
                link(nc.vector.tensor_reduce(picked_sum[:], picked[:], AX.X, ALU.add), g)
                link(nc.vector.tensor_scalar(picked_eps[:], picked_sum[:], TOPK_EPS, None, ALU.add), g)
                link(nc.vector.reciprocal(picked_inv[:], picked_eps[:]), g)
                nc.vector.tensor_scalar(combine_scale[:], picked_inv[:], ROUTED_SCALE, None, ALU.mult).then_inc(routed, 1)

            def attend(g):
                dve.wait_ge(pi_ready, after(g))
                for b in range(BPG):
                    ins = nc.vector.tensor_tensor_reduce(out=batch(weighted[:], b), in0=batch(w_sq[:], b), in1=batch(pi_bc[:], b),
                                                         scale=1.0, scalar=0.0, op0=ALU.mult, op1=ALU.add,
                                                         accum_out=dots[:, b:b + 1])
                link(ins, g)
                link(nc.vector.scalar_tensor_tensor(attn_den[:], pi_sum[:], PI_EPS, dots[:], ALU.add, ALU.add), g)
                link(nc.vector.reciprocal(attn_inv[:], attn_den[:]), g)
                link(nc.vector.scalar_tensor_tensor(attn[:], pi_sum[:], PI_EPS, attn_inv[:], ALU.add, ALU.mult), g)
                if not early(g, 2):
                    dve.wait_ge(down_done, count(shift(g, -2), NT, NT))
                for b in range(BPG):
                    ins = nc.vector.scalar_tensor_tensor(batch(attn_out[:, g[1] % 2], b), batch(ps_w[:], b), attn[:, b:b + 1],
                                                         batch(pi_bc[:], b), ALU.mult, ALU.mult)
                ins.then_inc(attn_ready, 1)
                assert step[0] == dve_per_group, step[0]

            def finish(g):
                dve.wait_ge(yT_ready, after(g))
                dve.wait_ge(x_res_loaded[g[1] % 2], loads(g))
                if not early(g, 2):
                    dve.wait_ge(stored[g[1] % 2], loads(shift(g, -2)))
                nc.vector.tensor_tensor(result[:, g[1] % 2], ps_x[:], x_res[:, g[1] % 2], ALU.add).then_inc(result_ready, 1)

            def rest_hidden(g, t):
                m = rows(t)
                dve.wait_ge(hid_hi_ready, count(g, NT, t + 1))
                if not (early(g, 1) and t < SPLIT_RING):
                    dve.wait_ge(down_done, count(g, NT, t + 1 - SPLIT_RING))
                r = t % SPLIT_RING
                nc.vector.tensor_tensor(hid_lo[0:m, r], hidden[0:m, t % RING], hid_hi[0:m, r], ALU.subtract).then_inc(hid_lo_ready, 1)

            def powers(c):
                setup_link(nc.vector.tensor_scalar(clamped[:, c], max_all[:, c], 2.0 ** -30, None, ALU.max))
                setup_link(nc.vector.tensor_scalar(power[:, c].bitcast(U32), clamped[:, c].bitcast(U32), EXP_MASK, None, ALU.bitwise_and))
                nc.vector.tensor_scalar(alpha[:, c].bitcast(U32), power[:, c].bitcast(U32), -1.0, over(14), ALU.mult, ALU.add)
                return nc.vector.tensor_scalar(inv_alpha[:, c], power[:, c], 2.0 ** -14, None, ALU.mult)

            def largest(k, ap):
                return nc.vector.tensor_reduce(maxima[:, k:k + 1], ap, AX.X, ALU.max, apply_absolute_value=True)

            def low_half(lo, hi, raw, k):
                nc.vector.scalar_tensor_tensor(lo[:, 0:FS], raw[:, 0:FS], alpha[:, k:k + 1], hi[:, 0:FS],
                                               ALU.mult, ALU.subtract).then_inc(weights_ready, 1)

            def low_half_routed(lo, hi, raw, k):
                nc.vector.scalar_tensor_tensor(routed_tiles(lo), routed_columns(raw), alpha[:, k:k + 1], routed_tiles(hi),
                                               ALU.mult, ALU.subtract).then_inc(weights_ready, 1)

            nc.vector.memset(down_raw[PART:P, FS - PART:SH * P], 0.0)
            nc.vector.memset(maxima[:], 0.0)
            statistics((0, 0))
            statistics_written((0, 0))
            mean_variance()
            dve.wait_ge(small_loaded, 16 * 2)
            dve.wait_ge(consts_done, 1)
            nc.vector.tensor_tensor(head_sel[:], head_sel[:], temp_bc[:], ALU.mult)
            normalise((0, 0))
            dve.wait_ge(gate_loaded, 32)
            largest(GATE, gate_raw[:])
            dve.wait_ge(projections_loaded, 48)
            nc.vector.tensor_reduce(maxima[0:E, ROUTER:ROUTER + 1], router_raw[:], AX.X, ALU.max, apply_absolute_value=True)
            largest(QKV, qkv_raw[:])
            dve.wait_ge(up_loaded, 32)
            largest(UP, up_raw[:]).then_inc(maxima_ready, 1)
            rest_x((0, 0))
            dve.wait_ge(maxima_spread, 1)
            setup_link(powers(slice(QKV, DOWN)))
            setup_link(nc.vector.tensor_scalar(gate_pow[:], power[:, GATE:GATE + 1], 2.0 ** -8, None, ALU.max))
            nc.vector.tensor_scalar(beta[:].bitcast(U32), gate_pow[:].bitcast(U32), -1.0, over(-17), ALU.mult,
                                    ALU.add).then_inc(scales_ready, 1)
            dve.wait_ge(transposes_taken, 1)
            nc.vector.tensor_scalar(qkv_hi[:], qkvT[:], alpha[:, QKV:QKV + 1], None, ALU.mult)
            setup_link(nc.vector.tensor_scalar(router_hi[:], routerT[:], alpha[:, ROUTER:ROUTER + 1], None, ALU.mult))
            nc.vector.scalar_tensor_tensor(qkv_lo[:], qkvT[:], alpha[:, QKV:QKV + 1], qkv_hi[:], ALU.mult, ALU.subtract)
            nc.vector.scalar_tensor_tensor(router_lo[:], routerT[:], alpha[:, ROUTER:ROUTER + 1], router_hi[:], ALU.mult,
                                           ALU.subtract).then_inc(projections_ready, 1)
            dve.wait_ge(weights_hi, 1)
            low_half(gate_lo, gate_hi, gate_raw, GATE)
            dve.wait_ge(weights_hi, 2)
            low_half(up_lo, up_hi, up_raw, UP)
            statistics((0, 1))
            statistics_written((0, 1))
            mean_variance()
            head_scales((0, 0))
            normalise((0, 1))
            shift_logits((0, 0))
            dve.wait_ge(weights_hi, 3)
            low_half_routed(gate_lo, gate_hi, gate_raw, GATE)

            def down_scales():
                dve.wait_ge(maxima_spread, 2)
                setup_link(powers(slice(DOWN, 5)))
                setup_link(nc.vector.tensor_scalar(gamma[:], beta[:], alpha[:, UP:UP + 1], alpha[:, DOWN:DOWN + 1], ALU.mult, ALU.mult))
                setup_link(nc.vector.tensor_scalar(neg_gamma_q[:], gamma[:], inv_alpha[:, QKV:QKV + 1], -1.0, ALU.mult, ALU.mult))
                setup_link(nc.vector.tensor_scalar(gate_pow[:], gate_pow[:], inv_alpha[:, UP:UP + 1], inv_alpha[:, DOWN:DOWN + 1],
                                                   ALU.mult, ALU.mult))
                nc.vector.tensor_scalar(woutT[:], woutT_raw[:], neg_gamma_q[:, 0:1], None, ALU.mult)
                nc.vector.tensor_scalar(inv_gamma[:], gate_pow[:], 2.0 ** 17, None, ALU.mult).then_inc(down_scales_ready, 1)

            def body(g):
                for t in range(NT):
                    n = g[1] * NT + t
                    m = rows(t)
                    if t == LAG + 1 and not early(g, 1):
                        finish(shift(g, -1))
                    if ahead_of(g, 1):
                        if t == slot(g, 'rest_x'):
                            rest_x(shift(g, 1))
                        if t == slot(g, 'head_scales'):
                            head_scales(shift(g, 1))
                        if t == slot(g, 'shift_logits'):
                            shift_logits(shift(g, 1))
                        if t == slot(g, 'rank_experts'):
                            rank_experts(shift(g, 1))
                        if t == slot(g, 'route'):
                            route(shift(g, 1))
                        if t == slot(g, 'attend'):
                            attend(shift(g, 1))
                    if ahead_of(g, 2):
                        if t == slot(g, 'statistics'):
                            statistics(shift(g, 2))
                        if t == slot(g, 'statistics') + 1:
                            statistics_written(shift(g, 2))
                        if t == slot(g, 'normalise'):
                            normalise(shift(g, 2))
                    if early(g, 1):
                        if t == OWN['largest_down']:
                            dve.wait_ge(down_loaded, 48)
                            largest(DOWN, down_raw[:]).then_inc(maxima_ready, 1)
                        if t == OWN['down_scales']:
                            down_scales()
                        if t == OWN['down_lo']:
                            dve.wait_ge(weights_hi, 5)
                            nc.vector.scalar_tensor_tensor(down_lo[:], down_raw[:], alpha[:, DOWN:DOWN + 1], down_hi[:], ALU.mult,
                                                           ALU.subtract).then_inc(weights_ready, 1)
                        if t == OWN['rank_experts']:
                            rank_experts(g)
                        if t == OWN['route']:
                            route(g)
                        if t == OWN['attend']:
                            attend(g)
                    dve.wait_ge(silu_ready, count(g, NT, t + 1))
                    dve.wait_ge(up_ready, count(g, NT, t + 1))
                    if not (early(g, 1) and t < RING):
                        last = back(g, t, RING)
                        dve.wait_ge(hid_hi_ready, count(last[0], NT, last[1] + 1))
                        if last[1] in POOL_REST:
                            rest_taken(dve, *last)
                    nc.vector.scalar_tensor_tensor(hidden[0:m, t % RING], act_gate[0:m, n % GATE_RING], beta[0:m, 0:1],
                                                   ps_up[0:m, n % 2], ALU.mult, ALU.mult).then_inc(hid_ready, 1)
                    last = back(g, t, LO_LAG)
                    if last[1] not in POOL_REST and not (early(g, 1) and t < LO_LAG):
                        rest_hidden(*last)
                    if t == slot(g, 'statistics') + 1 and ahead_of(g, 2):
                        mean_variance()

            run(dve, body)
            for t in range(NT - LO_LAG, NT):
                rest_hidden((0, G - 1), t)
            finish((0, G - 1))

        @block.tensor
        def _(pe):
            def three(out_ap, hi, lo, m_hi, m_lo, start, stop):
                nc.tensor.matmul(out_ap, hi, m_hi, start=start, stop=False)
                nc.tensor.matmul(out_ap, hi, m_lo, start=False, stop=False)
                return nc.tensor.matmul(out_ap, lo, m_hi, start=False, stop=stop)

            def transpose_x(g):
                pe.wait_ge(xn_ready, after(g))
                if early(g, 2) and not early(g, 1):
                    pe.wait_ge(lo_x_ready, after(g, 0))
                elif not early(g, 1):
                    pe.wait_ge(pi_ready, after(g, 0))
                for j in range(TJ):
                    ins = nc.tensor.transpose(ps_x[:, j * P:(j + 1) * P], xn[:, j], ident[:])
                ins.then_inc(xT_ready, 1)

            def project_w(g):
                q = g[1] % 2
                pe.wait_ge(lo_x_ready, after(g))
                if not early(g, 1):
                    pe.wait_ge(combine_ready, after(g, 0))
                    pe.wait_ge(attn_ready, after(g, 0))
                at = TJ * BPG * H
                for j in range(TJ):
                    c = slice(j * P, (j + 1) * P)
                    o = ps_s[:, at + j * E:at + (j + 1) * E]
                    nc.tensor.matmul(o, xT_hi[:, q, c], router_hi[:], start=True, stop=False)
                    nc.tensor.matmul(o, xT_hi[:, q, c], router_lo[:], start=False, stop=False)
                    nc.tensor.matmul(o, xT_lo[:, q, c], router_hi[:], start=False, stop=True)
                three(ps_w[:], qkv_hi[:], qkv_lo[:], xT_hi[:, q], xT_lo[:, q], True, True).then_inc(w_ready, 1)

            def head_logits(g):
                pe.wait_ge(head_scaled_ready, after(g))
                for j in range(TJ):
                    w = BPG * H
                    ins = nc.tensor.matmul(ps_s[:, j * w:(j + 1) * w], w_sq[:, j * P:(j + 1) * P],
                                           head_scaled[:].rearrange("p b h -> p (b h)"), start=True, stop=True)
                ins.then_inc(logits_ready, 1)

            def spread(g):
                pe.wait_ge(wide_ready, after(g))
                if early(g, 1):
                    pe.wait_ge(lo_x_ready, after(g, 2))
                elif not early(g, 2):
                    pe.wait_ge(result_ready, after(g, -1))
                for j in range(TJ):
                    c = slice(j * P, (j + 1) * P)
                    nc.tensor.transpose(ps_x[:, c], pi_wide[:, j].rearrange("p h d -> p (h d)"), ident[:])
                    ins = nc.tensor.transpose(ps_s[:, c], combine_wide[:, j].rearrange("p e f -> p (e f)"), ident[:])
                ins.then_inc(spread_ready, 1)

            def down(g, t):
                m = rows(t)
                r = t % SPLIT_RING
                c = slice(t * P, (t + 1) * P)
                rest_taken(pe, g, t)
                if t == 0 and not early(g, 1):
                    pe.wait_ge(y_taken, after(g, 0))
                if t == NT - 2:
                    pe.wait_ge(attn_ready, after(g))
                    nc.tensor.matmul(ps_y[:], woutT[:], attn_out[:, g[1] % 2], start=False, stop=False)
                three(ps_y[:], down_hi[0:m, c], down_lo[0:m, c], hid_hi[0:m, r], hid_lo[0:m, r],
                      t == 0, t == NT - 1).then_inc(down_done, 1)

            def transpose_y(g):
                pe.wait_ge(y_taken, after(g))
                if ahead_of(g, 1):
                    pe.wait_ge(lo_x_ready, after(shift(g, 1)))
                for j in range(TJ):
                    ins = nc.tensor.transpose(ps_x[:, j * P:(j + 1) * P], yT[:, j * P:(j + 1) * P], ident[:])
                ins.then_inc(yT_ready, 1)

            pe.wait_ge(consts_done, 1)
            pe.wait_ge(projections_loaded, 16 * 3)
            nc.tensor.transpose(ps_w[:, 0:P], qkv_raw[:], ident[:])
            nc.tensor.transpose(ps_w[:, P:2 * P], out_raw[:], ident[:])
            nc.tensor.transpose(ps_w[:, 2 * P:2 * P + E], router_raw[:], ident[0:E, 0:E]).then_inc(setup_transposed, 1)
            transpose_x((0, 0))
            pe.wait_ge(projections_ready, 1)
            project_w((0, 0))

            def gate(g, t):
                c, m, n = slice(t * P, t * P + rows(t)), rows(t), g[1] * NT + t
                if not (early(g, 1) and t < 2):
                    pe.wait_ge(silu_ready, count(g, NT, t - 1))
                three(ps_gate[0:m, n % 2], gate_hi[:, c], gate_lo[:, c], xT_hi[:, g[1] % 2], xT_lo[:, g[1] % 2],
                      True, True).then_inc(gate_ready, 1)

            def up(g, t):
                c, m, n = slice(t * P, t * P + rows(t)), rows(t), g[1] * NT + t
                if not (early(g, 1) and t < 2):
                    pe.wait_ge(hid_ready, count(g, NT, t - 1))
                three(ps_up[0:m, n % 2], up_hi[:, c], up_lo[:, c], xT_hi[:, g[1] % 2], xT_lo[:, g[1] % 2],
                      True, True).then_inc(up_ready, 1)

            def body(g):
                for t in range(NT):
                    if early(g, 1) and t == 0:
                        pe.wait_ge(weights_ready, 2)
                    if early(g, 1) and t == SH:
                        pe.wait_ge(weights_ready, 3)
                    if early(g, 1) and t == SH + 1:
                        pe.wait_ge(pool_weights_ready, 1)
                    gate(g, t)
                    if t >= 1:
                        up(g, t - 1)
                    elif not early(g, 1):
                        up(shift(g, -1), NT - 1)
                    if early(g, 1) and t == LAG:
                        pe.wait_ge(weights_ready, 4)
                    if t >= LAG:
                        down(g, t - LAG)
                    elif not early(g, 1):
                        down(shift(g, -1), t + NT - LAG)
                    if ahead_of(g, 1):
                        if t == slot(g, 'transpose_x'):
                            transpose_x(shift(g, 1))
                        if t == slot(g, 'project_w'):
                            project_w(shift(g, 1))
                        if t == slot(g, 'head_logits'):
                            head_logits(shift(g, 1))
                        if t == slot(g, 'spread'):
                            spread(shift(g, 1))
                    if t == own(g, 'head_logits'):
                        head_logits(g)
                    if t == own(g, 'spread'):
                        spread(g)
                    if t == LAG and not early(g, 1):
                        transpose_y(shift(g, -1))

            run(pe, body)
            up((0, G - 1), NT - 1)
            for t in range(NT - LAG, NT):
                down((0, G - 1), t)
            transpose_y((0, G - 1))


_INS = ['L0_attn_x', 'L0_attn_Wqkv', 'L0_attn_temp', 'L0_attn_Wout', 'L0_attn_bout', 'L0_ffn_gate_w', 'L0_ffn_w_gate',
        'L0_ffn_w_up', 'L0_ffn_w_down', 'L0_ffn_sw_gate', 'L0_ffn_sw_up', 'L0_ffn_sw_down']


def kernel(**inputs):
    import numpy as np
    import concourse.bacc as bacc
    from concourse.bass_utils import run_bass_kernel_spmd

    nc = bacc.Bacc("TRN2", target_bir_lowering=False, num_devices=1)
    arrays, args = {}, []
    for name in _INS:
        a = np.ascontiguousarray(inputs[name])
        arrays[f"in_{name}"] = a
        args.append(nc.dram_tensor(f"in_{name}", a.shape, mybir.dt.from_np(a.dtype), kind="ExternalInput").ap())
    out = nc.dram_tensor("out", arrays["in_L0_attn_x"].shape, F32, kind="ExternalOutput").ap()
    attn_moe_kernel(nc, *args, out)
    r = run_bass_kernel_spmd(nc, [arrays], core_ids=[0])
    return r.results[0]["out"]
```
